# Optimizing a Trainium2 kernel written in Bass

```python
import numpy as np
import jax
import jax.numpy as jnp

def _softmax(x, axis=-1):
    return jax.nn.softmax(x, axis=axis)
def _gelu(x):
    return jax.nn.gelu(x, approximate=True)
def _silu(x):
    return jax.nn.silu(x)
def _sigmoid(x):
    return jax.nn.sigmoid(x)
def _layernorm(x, axis=-1, eps=1e-5):
    m = jnp.mean(x, axis=axis, keepdims=True)
    v = jnp.var(x, axis=axis, keepdims=True)
    return (x - m) / jnp.sqrt(v + eps)
def _scatter_add(tgt, idx, src, axis=0):
    return tgt.at[idx].add(src)
def _segment_sum(src, seg, n):
    return jax.ops.segment_sum(src, seg, n)

kernel_name = 'mk_conv_seq_d1_conv_nchw512_e7a863'

def setup_inputs(seed: int = 0):
    np.random.seed(seed)
    _w = jnp.asarray
    def _rec_inputs():
        import jax
        import jax.numpy as jnp
        _gk = jax.random.key(seed)
        x = -0.0001732 + 1 * jax.random.normal(jax.random.fold_in(_gk, 1), (4, 512, 48, 48), jnp.float32)
        return x
    x = _rec_inputs()
    def _L0_conv_setup():
        import jax, jax.numpy as jnp
        import numpy as np
        import math
        C = 512
        N_HEADS = 8
        N_GROUPS = 32
        EPS = 1e-05
        key = jax.random.key(seed)
        k1, k2, k3 = jax.random.split(key, 3)
        B, H, W = (4, 48, 48)
        x = jax.random.normal(k1, (B, C, H, W), dtype=jnp.float32)
        gn_w = jnp.ones((C,), jnp.float32)
        gn_b = jnp.zeros((C,), jnp.float32)
        qkv_w = jax.random.normal(k2, (3 * C, C), jnp.float32) * (1.0 / math.sqrt(C))
        qkv_b = jnp.zeros((3 * C,), jnp.float32)
        proj_w = jax.random.normal(k3, (C, C), jnp.float32) * (1.0 / math.sqrt(C))
        proj_b = jnp.zeros((C,), jnp.float32)
        return {'x': x, 'gn_w': gn_w, 'gn_b': gn_b, 'qkv_w': qkv_w, 'qkv_b': qkv_b, 'proj_w': proj_w, 'proj_b': proj_b}
    _L0_conv_all = _L0_conv_setup()
    _L0_conv_in = {k: v for k, v in _L0_conv_all.items() if k in ('gn_w', 'gn_b', 'qkv_w', 'qkv_b', 'proj_w', 'proj_b', )}
    del _L0_conv_all

    return {
        "x": x,
        "L0_conv_gn_w": _L0_conv_in["gn_w"],
        "L0_conv_gn_b": _L0_conv_in["gn_b"],
        "L0_conv_qkv_w": _L0_conv_in["qkv_w"],
        "L0_conv_qkv_b": _L0_conv_in["qkv_b"],
        "L0_conv_proj_w": _L0_conv_in["proj_w"],
        "L0_conv_proj_b": _L0_conv_in["proj_b"],
    }

def reference(x, L0_conv_gn_w, L0_conv_gn_b, L0_conv_qkv_w, L0_conv_qkv_b, L0_conv_proj_w, L0_conv_proj_b):
    import jax
    import jax.numpy as jnp
    def _L0_conv_ref(x, gn_w, gn_b, qkv_w, qkv_b, proj_w, proj_b):
        import jax, jax.numpy as jnp
        import numpy as np
        import math
        C = 512
        N_HEADS = 8
        N_GROUPS = 32
        EPS = 1e-05
        b, c, h, w = x.shape
        T = h * w
        xf = x.reshape(b, c, T)
        xg = xf.reshape(b, N_GROUPS, c // N_GROUPS, T)
        mean = xg.mean(axis=(2, 3), keepdims=True)
        var = xg.var(axis=(2, 3), keepdims=True)
        xn = (xg - mean) * jax.lax.rsqrt(var + EPS)
        xn = xn.reshape(b, c, T) * gn_w[None, :, None] + gn_b[None, :, None]
        qkv = jnp.einsum('oc,bct->bot', qkv_w, xn) + qkv_b[None, :, None]
        ch = c // N_HEADS
        qkv = qkv.reshape(b * N_HEADS, 3 * ch, T)
        q, k, v = jnp.split(qkv, 3, axis=1)
        scale = 1.0 / math.sqrt(math.sqrt(ch))
        weight = jnp.einsum('bct,bcs->bts', q * scale, k * scale)
        weight = jax.nn.softmax(weight.astype(jnp.float32), axis=-1).astype(qkv.dtype)
        a = jnp.einsum('bts,bcs->bct', weight, v).reshape(b, c, T)
        hout = jnp.einsum('oc,bct->bot', proj_w, a) + proj_b[None, :, None]
        return (xn + hout).reshape(b, c, h, w)

    def _gn(v, G=32, eps=1e-5):
        B_, C_, H_, W_ = v.shape
        g = v.reshape(B_, G, C_ // G, H_, W_)
        m = jnp.mean(g, axis=(2, 3, 4), keepdims=True)
        s = jnp.var(g, axis=(2, 3, 4), keepdims=True)
        return ((g - m) / jnp.sqrt(s + eps)).reshape(v.shape)

    def _ln_c(v, eps=1e-6):
        m = jnp.mean(v, axis=1, keepdims=True)
        s = jnp.var(v, axis=1, keepdims=True)
        return (v - m) / jnp.sqrt(s + eps)

    def _ln_t(v, eps=1e-5):
        m = jnp.mean(v, axis=-1, keepdims=True)
        s = jnp.var(v, axis=-1, keepdims=True)
        return (v - m) / jnp.sqrt(s + eps)

    def _to_tokens(v):
        B_, C_, H_, W_ = v.shape
        return v.reshape(B_, C_, H_ * W_).transpose(0, 2, 1)
    def _from_tokens(t, like):
        B_, C_, H_, W_ = like.shape
        return t.transpose(0, 2, 1).reshape(B_, C_, H_, W_)

    x = _L0_conv_ref(x, L0_conv_gn_w, L0_conv_gn_b, L0_conv_qkv_w, L0_conv_qkv_b, L0_conv_proj_w, L0_conv_proj_b)
    return x


_drawn_inputs = setup_inputs


def setup_inputs(seed=0):
    import zlib

    import numpy as np

    out = dict(_drawn_inputs(seed))
    spreads = {'L0_conv_gn_w': (1.0, 0.2),
     'L0_conv_gn_b': (0.0, 0.1),
     'L0_conv_qkv_b': (0.0, 0.1),
     'L0_conv_proj_b': (0.0, 0.1)}
    factors = {}
    for name, (base, spread) in spreads.items():
        noise = np.random.default_rng([zlib.crc32(name.encode()), seed]).standard_normal(out[name].shape)
        drawn = base * np.exp(spread * noise) if base else spread * noise
        out[name] = jnp.asarray(drawn.astype(out[name].dtype))
    for name, factor in factors.items():
        out[name] = (out[name] * factor).astype(out[name].dtype)
    return out
```

```python
import concourse.bass as bass
from concourse import mybir
from contextlib import ExitStack


def attention_block_program(nc, x, gn_w, gn_b, wqkv_t, bqk, bv, wproj_t, bproj, att, out):
    fp32 = mybir.dt.float32
    fp32r = mybir.dt.float32r
    ALU = mybir.AluOpType
    ACT = mybir.ActivationFunctionType
    AX = mybir.AxisListType

    B, C, T = x.shape
    H = 8
    D = C // H
    CT = C // 128
    GROUP = C // 32
    EPS = 1e-5
    QK_SCALE = float(D) ** -0.25
    PAIRS = H // 2
    N = 384
    QB = 2 * N
    BLOCKS = T // QB
    KT = T // 128
    CH = T // N
    STEPS = BLOCKS * KT
    PSTEPS = 2 * STEPS
    UNITS = KT * BLOCKS
    VG = KT // 3
    RING = 4
    ADDS = KT // 2 - 1
    FINS = 2 * BLOCKS
    PRIMED = 1
    PJ = CH * CT

    def plan(last):
        before = [[] for _ in range(PSTEPS)]
        after = [[] for _ in range(PSTEPS)]
        for par in range(2):
            t0 = par * STEPS
            for c in range(CH):
                before[t0 + 1 + c].append(("prep", c))
            first, final = 9, 46
            seen = 0
            for s in range(first, final + 1):
                upto = UNITS * (s - first + 1) // (final - first + 1)
                for i, u in enumerate(range(seen, upto)):
                    (before if i == 0 else after)[t0 + s].append(("aux", u))
                seen = upto
            before[t0 + 48].append(("maxrow", 0))
            for j in range(BLOCKS):
                t = t0 + (j + 1) * KT + 2
                if t < PSTEPS:
                    before[t].append(("finish", par * BLOCKS + j))
        for g, t in enumerate((49, 50, 51, 52, 53, 53)):
            before[STEPS + t].append(("v", g))
        if last:
            for i in range(CT):
                before[10 + 6 * i].append(("stats", i))
                before[40 + 3 * i].append(("normalize", i))
            before[33].append(("groupmean", 0))
            before[35].append(("groupvar", 0))
            before[36].append(("sqrt", 0))
            before[37].append(("coefs", 0))
        return before, after

    PLANS = {last: plan(last) for last in (False, True)}
    ON_MISC = ("prep", "v", "maxrow", "finish", "groupmean", "groupvar")

    def misc_order(last):
        order = {}
        before, _ = PLANS[last]
        for t in range(PSTEPS):
            for kind, i in before[t]:
                if kind in ON_MISC:
                    order[(t // STEPS, kind, i) if kind in ("prep", "maxrow") else (kind, i)] = len(order)
        order[("finish", FINS - 1)] = len(order)
        return order

    MISC_AT = {last: misc_order(last) for last in (False, True)}
    MISC_PRO = 3 + CH + VG + 1
    MISC_PAIR = len(MISC_AT[False])

    def misc_base(b, p):
        return MISC_PRO + b * (PAIRS * MISC_PAIR + 2) + p * MISC_PAIR

    def key(par, kind, i):
        return (par, kind, i) if kind in ("prep", "maxrow") else (kind, i)

    with ExitStack() as ctx:
        def sb(name, shape, dt=fp32):
            return ctx.enter_context(nc.sbuf_tensor(name, shape, dt))

        def sem(name):
            return ctx.enter_context(nc.semaphore(name))

        q_hi_hi = [sb(f"q_hi_hi{i}", [128, T], fp32r) for i in range(2)]
        q_lo_max = [sb(f"q_lo_max{i}", [D + 1, T], fp32r) for i in range(2)]
        k_hi_lo = [sb(f"k_hi_lo{i}", [128, T], fp32r) for i in range(2)]
        k_hi_one = [sb(f"k_hi_one{i}", [D + 1, T], fp32r) for i in range(2)]
        xn = sb("xn", [128, CT, T])
        xtile = sb("xtile", [128, T])
        v_even = sb("v_even", [128, KT, D])
        v_odd = sb("v_odd", [128, KT, D])
        v_odd_next = sb("v_odd_next", [128, KT, D])
        probs = sb("probs", [128, RING * QB])
        denom = sb("denom", [128, 2, 2, QB])
        qk_full = sb("qk_full", [D, 2, N])
        o_raw = sb("o_raw", [128, N])
        recip = sb("recip", [128, N])
        o_norm = sb("o_norm", [128, N])
        wqk = [sb(f"wqk{i}", [128, CT, 128]) for i in range(2)]
        wv = sb("wv", [128, CT, 128])
        wproj = sb("wproj", [128, CT, C])
        att_in = [sb(f"att_in{i}", [128, CT, N]) for i in range(2)]
        ident = sb("ident", [128, 128])
        groups = sb("groups", [128, 128])
        ones = sb("ones", [128, D])
        maxima = sb("maxima", [128, UNITS])
        neg_max = sb("neg_max", [128, KT])
        max_rows = sb("max_rows", [KT, 128], fp32r)
        bqk_s = sb("bqk_s", [128, H])
        spare = sb("spare", [128, 1])
        head_bias = sb("head_bias", [128, 1])
        small = sb("small", [128, 64])
        stats = sb("stats", [128, CH, 6])

        def cols(n):
            return small[:, CT * n:CT * (n + 1)]

        gw, gb, pb, bvs = cols(0), cols(1), cols(2), cols(3)
        next_a, next_b, res_a, res_b = cols(4), cols(5), cols(6), cols(7)
        dev, gmean, tmp, gvar, root, inv = cols(8), cols(9), cols(10), cols(11), cols(12), cols(13)
        meanvar = sb("meanvar", [128, CT, 2])

        def xres(i):
            return probs[:, 2 * QB * i:2 * QB * (i + 1)].rearrange("p (o n) -> p o n", n=N)

        proj_sb = denom[:, :, :, :].rearrange("p a e (h n) -> p (a e h) n", n=N)

        scores = ctx.enter_context(nc.psum_tensor("scores", [128, 2, 2, 512], fp32))
        aux = ctx.enter_context(nc.psum_tensor("aux", [128, 2, 512], fp32))
        oacc = ctx.enter_context(nc.psum_tensor("oacc", [128, 512], fp32))
        misc = ctx.enter_context(nc.psum_tensor("misc", [128, 512], fp32))

        consts_in = sem("consts_in")
        wproj_in = sem("wproj_in")
        wqk_in = [sem(f"wqk_in{i}") for i in range(2)]
        wv_in = sem("wv_in")
        x_in = sem("x_in")
        consts_made = sem("consts_made")
        stats_done = sem("stats_done")
        dev_ready = sem("dev_ready")
        root_ready = sem("root_ready")
        coefs_ready = sem("coefs_ready")
        xn_ready = sem("xn_ready")
        chain = sem("chain")
        shift_ready = sem("shift_ready")
        masks_filled = sem("masks_filled")
        res_coefs_ready = sem("res_coefs_ready")
        misc_full = sem("misc_full")
        misc_free = sem("misc_free")
        hi_ready = sem("hi_ready")
        lo_ready = sem("lo_ready")
        copies_ready = sem("copies_ready")
        bias_ready = sem("bias_ready")
        aux_full = sem("aux_full")
        max_done = sem("max_done")
        neg_ready = sem("neg_ready")
        maxrow_in = sem("maxrow_in")
        v_ready = sem("v_ready")
        v_odd_ready = sem("v_odd_ready")
        scores_full = sem("scores_full")
        probs_ready = sem("probs_ready")
        pv_done = sem("pv_done")
        added = [sem("added_dve"), sem("added_pool")]
        o_saved = sem("o_saved")
        recip_ready = sem("recip_ready")
        o_normed = sem("o_normed")
        att_out = sem("att_out")
        att_back = [sem(f"att_back{i}") for i in range(2)]
        xres_in = [sem(f"xres_in{i}") for i in range(2)]
        proj_full = sem("proj_full")
        proj_saved = sem("proj_saved")
        out_ready = sem("out_ready")
        stored = [sem(f"stored{i}") for i in range(2)]

        block = ctx.enter_context(nc.Block())

        def adds_by(t):
            kt = t % KT
            return t // KT * ADDS + max(1, kt // 2)

        def pair_no(b, p):
            return b * PAIRS + p

        @block.sync
        def _(sp):
            def load_wqk(h, buf):
                src = wqkv_t.rearrange("(k c) h n -> c k h n", c=128)[:, :, bass.ds(h, 1), 0:2 * D]
                sp.dma_start(wqk[buf][:, :, :], src.rearrange("c k h n -> c k (h n)")).then_inc(wqk_in[buf], 16)

            def load_wv(p):
                for i in range(2):
                    src = wqkv_t.rearrange("(k c) h n -> c k h n", c=128)[:, :, bass.ds(2 * p + i, 1), 2 * D:3 * D]
                    sp.dma_start(wv[:, :, i * D:(i + 1) * D],
                                 src.rearrange("c k h n -> c k (h n)")).then_inc(wv_in, 16)

            def load_x(b, i):
                sp.dma_start(xtile[:, :], x[bass.ds(b, 1), i * 128:(i + 1) * 128, :]
                             .rearrange("b c t -> (b c) t")).then_inc(x_in, 16)

            def copy_chunk(c, buf, n):
                cs = slice(c * N, (c + 1) * N)
                sp.wait_ge(hi_ready, n)
                sp.dma_start(q_hi_hi[buf][D:2 * D, cs].bitcast(fp32),
                             q_hi_hi[buf][0:D, cs].bitcast(fp32)).then_inc(copies_ready, 16)
                sp.dma_start(k_hi_one[buf][0:D, cs].bitcast(fp32),
                             k_hi_lo[buf][0:D, cs].bitcast(fp32)).then_inc(copies_ready, 16)

            def put_max_row(buf, misc_n):
                sp.wait_ge(misc_free, misc_n)
                sp.dma_start(q_lo_max[buf][D:D + 1, :].bitcast(fp32).rearrange("o (t q) -> o t q", q=128),
                             max_rows[:, :].bitcast(fp32)).then_inc(maxrow_in, 16)

            def norm_load(b, i, k, second):
                if second:
                    if i:
                        sp.wait_ge(xn_ready, CT * k + i)
                    else:
                        sp.wait_ge(stats_done, CT * (k + 1))
                elif i:
                    sp.wait_ge(stats_done, CT * k + i)
                load_x(b, i)

            def put_block(b, p, j, g):
                par, blk = j // BLOCKS, j % BLOCKS
                sp.wait_ge(o_normed, PRIMED + FINS * g + j + 1)
                for half in range(2):
                    q0 = blk * QB + half * N
                    dst = att[bass.ds(p, 1), par * D:(par + 1) * D, q0:q0 + N].rearrange("a c t -> (a c) t")
                    sp.dma_start(dst, o_norm[half * D:(half + 1) * D, :]).then_inc(att_out, 16)

            def pair(b, p, last):
                g = pair_no(b, p)
                before, _ = PLANS[last]
                mb = misc_base(b, p)
                nb = (b + 1) % B
                if last:
                    sp.wait_ge(xn_ready, CT * (b + 1))
                    norm_load(nb, 0, b + 1, False)
                for t in range(PSTEPS):
                    par = t // STEPS
                    if t % STEPS == 10:
                        if par == 0:
                            sp.wait_ge(misc_full, mb + MISC_AT[last][(0, "prep", CH - 1)] + 1)
                            load_wqk(0 if last else 2 * p + 2, 0)
                            load_wv(0 if last else p + 1)
                        else:
                            sp.wait_ge(misc_full, mb + MISC_AT[last][(1, "prep", CH - 1)] + 1)
                            load_wqk(1 if last else 2 * p + 3, 1)
                    for kind, i in before[t]:
                        if kind == "prep":
                            copy_chunk(i, 1 - par, CH * (2 * g + par + 1) + i + 1)
                        elif kind == "maxrow":
                            put_max_row(1 - par, mb + MISC_AT[last][(par, kind, i)] + 1)
                        elif kind == "finish":
                            put_block(b, p, i, g)
                        elif kind == "stats" and i + 1 < CT:
                            norm_load(nb, i + 1, b + 1, False)
                        elif kind == "coefs":
                            norm_load(nb, 0, b + 1, True)
                        elif kind == "normalize" and i + 1 < CT:
                            norm_load(nb, i + 1, b + 1, True)
                if not last:
                    put_block(b, p, FINS - 1, g)

            def load_att(b, tc):
                i = tc % 2
                sp.dma_start(att_in[i][:, :, :], att[:, :, tc * N:(tc + 1) * N]
                             .rearrange("k c t -> c k t")).then_inc(att_back[i], 16)

            def chan(ap, b, tc):
                return ap[bass.ds(b, 1), :, tc * N:(tc + 1) * N].rearrange("b (k c) t -> c (b k) t", c=128)

            def projection(b):
                g = pair_no(b, PAIRS - 1)
                puts = 32 * FINS
                sp.wait_ge(att_out, PRIMED + puts * g + 32 * (FINS - 1))
                load_att(b, 0)
                load_att(b, 1)
                put_block(b, PAIRS - 1, FINS - 1, g)
                for tc in range(2):
                    sp.dma_start(xres(tc), chan(x, b, tc)).then_inc(xres_in[tc], 16)
                for tc in range(CH):
                    i = tc % 2
                    sp.wait_ge(out_ready, PRIMED + PJ * b + CT * (tc + 1))
                    sp.dma_start(chan(out, b, tc), xres(i)).then_inc(stored[i], 16)
                    if tc + 2 < CH:
                        if tc + 2 == 2 * (CH // 3):
                            sp.wait_ge(att_out, PRIMED + puts * (g + 1))
                        load_att(b, tc + 2)
                        sp.wait_ge(stored[i], PRIMED + 16 * (CH // 2 * b + tc // 2 + 1))
                        sp.dma_start(xres(i), chan(x, b, tc + 2)).then_inc(xres_in[i], 16)

            for s in (att_out, stored[0], stored[1]):
                sp.sem_inc(s, PRIMED)
            norm_load(0, 0, 0, False)
            load_wqk(0, 0)
            for dst, src in ((gw, gn_w), (gb, gn_b), (pb, bproj), (bvs, bv), (bqk_s[:, :], bqk)):
                sp.dma_start(dst, src).then_inc(consts_in, 16)
            for i in range(1, CT):
                norm_load(0, i, 0, False)
            sp.dma_start(wproj[:, :, :], wproj_t.rearrange("(k c) n -> c k n", c=128)).then_inc(wproj_in, 16)
            load_wqk(1, 1)
            load_wv(0)
            for i in range(CT):
                norm_load(0, i, 0, True)
            for c in range(CH):
                copy_chunk(c, 0, c + 1)
            put_max_row(0, MISC_PRO)
            with sp.Fori(0, B) as b:
                with sp.Fori(0, PAIRS - 1) as p:
                    pair(b, p, False)
                pair(b, PAIRS - 1, True)
                projection(b)
            for i in range(2):
                sp.wait_ge(stored[i], PRIMED + 16 * (CH // 2) * B)
            sp.wait_ge(att_out, PRIMED + 32 * FINS * PAIRS * B)
            sp.wait_ge(maxrow_in, 16 * (H * B + 1))
            for i in range(2):
                sp.wait_ge(wqk_in[i], 16 * (PAIRS * B + 1))
            sp.wait_ge(wv_in, 32 * (PAIRS * B + 1))

        @block.tensor
        def _(pe):
            mm = nc.tensor.matmul

            def prep(c, buf, misc_n, wait_w):
                if c == 0:
                    pe.wait_ge(wqk_in[buf], wait_w)
                pe.wait_ge(misc_free, misc_n)
                for k in range(CT):
                    last = mm(misc[:, 0:N], wqk[buf][:, k, :], xn[:, k, c * N:(c + 1) * N],
                              start=(k == 0), stop=(k == CT - 1))
                last.then_inc(misc_full, 1)

            def v_group(vg, misc_n, wait_w):
                if vg == 0:
                    pe.wait_ge(wv_in, wait_w)
                pe.wait_ge(misc_free, misc_n)
                for i in range(3):
                    tt = 3 * vg + i
                    for k in range(CT):
                        last = mm(misc[:, i * 128:(i + 1) * 128], xn[:, k, tt * 128:(tt + 1) * 128],
                                  wv[:, k, :], start=(k == 0), stop=(k == CT - 1))
                last.then_inc(misc_full, 1)

            def aux_unit(u, buf, head):
                qt, kc = u // BLOCKS, u % BLOCKS
                if u == 0:
                    pe.wait_ge(copies_ready, 32 * CH * (head + 1))
                    pe.wait_ge(lo_ready, CH * (head + 1))
                pe.wait_ge(max_done, UNITS * head + u)
                for half in range(2):
                    k0 = kc * QB + half * N
                    last = mm(aux[:, half, 0:N], q_hi_hi[buf][:, qt * 128:(qt + 1) * 128],
                              k_hi_lo[buf][:, k0:k0 + N], start=True, stop=True)
                last.then_inc(aux_full, 1)

            def max_row(n, misc_n):
                pe.wait_ge(neg_ready, n)
                pe.wait_ge(misc_free, misc_n)
                nc.tensor.transpose(misc[0:KT, 0:128], neg_max[:, :], ident[:, :]).then_inc(misc_full, 1)

            def group_mean(k, misc_n):
                pe.wait_ge(stats_done, CT * (k + 1))
                pe.wait_ge(misc_free, misc_n)
                mm(misc[:, 0:CT], groups[:, :], meanvar[:, :, 0], start=True, stop=True).then_inc(misc_full, 1)

            def group_var(k, misc_n):
                pe.wait_ge(dev_ready, k + 1)
                pe.wait_ge(misc_free, misc_n)
                mm(misc[:, 0:CT], groups[:, :], tmp, start=True, stop=True).then_inc(misc_full, 1)

            def finish(j, g, misc_n):
                for e in range(2):
                    pe.wait_ge(added[e], PRIMED + FINS * ADDS * g + ADDS * (j + 1))
                pe.wait_ge(misc_free, misc_n)
                for e in range(2):
                    for half in range(2):
                        last = mm(misc[half * D:(half + 1) * D, 0:N], ones[:, :],
                                  denom[:, j % 2, e, half * N:(half + 1) * N], start=(e == 0), stop=(e == 1))
                last.then_inc(misc_full, 1)

            def make_scores(t, g):
                par, s = t // STEPS, t % STEPS
                blk, kt = s // KT, s % KT
                if s == 0:
                    pe.wait_ge(maxrow_in, 16 * (2 * g + par + 1))
                pe.wait_ge(probs_ready, PRIMED + PSTEPS * g + max(0, t - 1))
                ks = slice(kt * 128, (kt + 1) * 128)
                for part, (kk, qq) in enumerate(((k_hi_lo, q_hi_hi), (k_hi_one, q_lo_max))):
                    for half in range(2):
                        q0 = blk * QB + half * N
                        last = mm(scores[:, t % 2, half, 0:N], kk[par][:, ks], qq[par][:, q0:q0 + N],
                                  start=(part == 0), stop=(part == 1))
                last.then_inc(scores_full, 1)

            def make_pv(t, g):
                par, s = t // STEPS, t % STEPS
                kt = s % KT
                if t == 0:
                    pe.wait_ge(v_ready, VG * (g + 1))
                if t == STEPS:
                    pe.wait_ge(v_odd_ready, g + 1)
                pe.wait_ge(probs_ready, PRIMED + PSTEPS * g + t + 1)
                if kt == 0:
                    pe.wait_ge(o_saved, PRIMED + FINS * g + t // KT)
                v = v_odd if par else v_even
                p0 = t % RING * QB
                for half in range(2):
                    last = mm(oacc[half * D:(half + 1) * D, 0:N], v[:, kt, :],
                              probs[:, p0 + half * N:p0 + (half + 1) * N], start=(kt == 0), stop=(kt == KT - 1))
                last.then_inc(pv_done, 1)

            def pair(b, p, last):
                g = pair_no(b, p)
                before, after = PLANS[last]
                mb = misc_base(b, p)
                pe.wait_ge(proj_saved, PRIMED + PJ * b)
                for t in range(PSTEPS):
                    par = t // STEPS
                    make_scores(t, g)
                    for kind, i in before[t]:
                        at = MISC_AT[last].get(key(par, kind, i), 0) + mb
                        if kind == "prep":
                            if last and par == 1 and i == 0:
                                pe.wait_ge(xn_ready, CT * (b + 2))
                            prep(i, 1 - par, at, 16 * (g + 2 if par else g + 1))
                        elif kind == "v":
                            v_group(i, at, 32 * (g + 2))
                        elif kind == "aux":
                            aux_unit(i, 1 - par, 2 * g + par + 1)
                        elif kind == "maxrow":
                            max_row(2 * g + par + 2, at)
                        elif kind == "finish":
                            finish(i, g, at)
                        elif kind == "groupmean":
                            group_mean(b + 1, at)
                        elif kind == "groupvar":
                            group_var(b + 1, at)
                    if t:
                        make_pv(t - 1, g)
                    for _, i in after[t]:
                        aux_unit(i, 1 - par, 2 * g + par + 1)
                make_pv(PSTEPS - 1, g)
                finish(FINS - 1, g, mb + MISC_AT[last][("finish", FINS - 1)])

            def projection(b):
                for tc in range(CH):
                    i = tc % 2
                    pe.wait_ge(att_back[i], 16 * (CH // 2 * b + tc // 2 + 1))
                    for ot in range(CT):
                        n = tc * CT + ot
                        if n >= 4:
                            pe.wait_ge(proj_saved, PRIMED + PJ * b + n - 3)
                        for k in range(CT):
                            last = mm(scores[:, n // 2 % 2, n % 2, 0:N], wproj[:, k, ot * 128:(ot + 1) * 128],
                                      att_in[i][:, k, :], start=(k == 0), stop=(k == CT - 1))
                        last.then_inc(proj_full, 1)

            pe.sem_inc(pv_done, PRIMED)
            pe.wait_ge(consts_made, 7)
            group_mean(0, 0)
            group_var(0, 1)
            pe.wait_ge(wproj_in, 16)
            pe.wait_ge(consts_in, 80)
            pe.wait_ge(misc_free, 2)
            for ot in range(CT):
                for k in range(CT):
                    last = mm(misc[:, ot:ot + 1], wproj[:, k, ot * 128:(ot + 1) * 128], bvs[:, k:k + 1],
                              start=(k == 0), stop=(k == CT - 1))
            last.then_inc(misc_full, 1)
            pe.wait_ge(xn_ready, CT)
            for c in range(CH):
                prep(c, 0, 3 + c, 16)
            for u in range(UNITS):
                aux_unit(u, 0, 0)
                if u % 9 == 4:
                    v_group(u // 9, 3 + CH + u // 9, 32)
            max_row(1, MISC_PRO - 1)
            with pe.Fori(0, B) as b:
                with pe.Fori(0, PAIRS - 1) as p:
                    pair(b, p, False)
                pair(b, PAIRS - 1, True)
                projection(b)

        @block.scalar
        def _(act):
            a = nc.scalar.activation

            def prep(c, buf, misc_n, heads, head):
                cs = slice(c * N, (c + 1) * N)
                bq, bk = head_bias[0:D, :], head_bias[D:2 * D, :]
                if c == 0:
                    a(head_bias[:, :], bqk_s[:, bass.ds(head, 1)], ACT.Copy).then_inc(bias_ready, 1)
                    act.wait_ge(bias_ready, heads + 1)
                act.wait_ge(misc_full, misc_n)
                a(q_hi_hi[buf][0:D, cs], misc[0:D, 0:N], ACT.Identity, scale=QK_SCALE, bias=bq)
                a(k_hi_lo[buf][0:D, cs], misc[D:2 * D, 0:N], ACT.Identity, scale=QK_SCALE,
                  bias=bk).then_inc(hi_ready, 1)
                act.wait_ge(lo_ready, CH * heads + c)
                a(qk_full[:, 0, :], misc[0:D, 0:N], ACT.Identity, scale=QK_SCALE, bias=bq)
                a(qk_full[:, 1, :], misc[D:2 * D, 0:N], ACT.Identity, scale=QK_SCALE,
                  bias=bk).then_inc(misc_free, 1)

            def v_group(vg, misc_n, copied):
                act.wait_ge(misc_full, misc_n)
                if vg == 0:
                    act.wait_ge(v_odd_ready, copied)
                m = misc[:, 0:3 * 128].rearrange("p (t h c) -> p h t c", t=3, h=2)
                a(v_even[:, 3 * vg:3 * vg + 3, :], m[:, 0], ACT.Copy).then_inc(v_ready, 1)
                a(v_odd_next[:, 3 * vg:3 * vg + 3, :], m[:, 1], ACT.Copy).then_inc(misc_free, 1)

            def max_row(misc_n, rows_sent):
                act.wait_ge(misc_full, misc_n)
                act.wait_ge(maxrow_in, rows_sent)
                a(max_rows[:, :], misc[0:KT, 0:128], ACT.Copy).then_inc(misc_free, 1)

            def sqrt(misc_n, k):
                act.wait_ge(misc_free, misc_n)
                a(root, gvar, ACT.Sqrt).then_inc(root_ready, 1)

            def save_o(j, g):
                act.wait_ge(pv_done, PRIMED + PSTEPS * g + KT * (j + 1))
                act.wait_ge(o_normed, PRIMED + FINS * g + j)
                a(o_raw[:, :], oacc[:, 0:N], ACT.Copy).then_inc(o_saved, 1)

            def pair(b, p, last):
                g = pair_no(b, p)
                before, _ = PLANS[last]
                mb = misc_base(b, p)
                for t in range(PSTEPS):
                    par = t // STEPS
                    act.wait_ge(pv_done, PRIMED + PSTEPS * g + max(0, t - RING + 1))
                    if t < RING:
                        if t == 0:
                            for e in range(2):
                                act.wait_ge(added[e], PRIMED + FINS * ADDS * g)
                    else:
                        act.wait_ge(added[t % 2], PRIMED + FINS * ADDS * g + adds_by(t - RING))
                    act.wait_ge(scores_full, PSTEPS * g + t + 1)
                    a(probs[:, t % RING * QB:(t % RING + 1) * QB].rearrange("p (h n) -> p h n", n=N),
                      scores[:, t % 2, :, 0:N], ACT.Exp).then_inc(probs_ready, 1)
                    if t == 3:
                        act.wait_ge(v_ready, VG * (g + 1))
                        act.wait_ge(misc_free, mb)
                        a(v_odd[:, :, :], v_odd_next[:, :, :], ACT.Copy).then_inc(v_odd_ready, 1)
                    for kind, i in before[t]:
                        at = MISC_AT[last].get(key(par, kind, i), 0) + mb + 1
                        if kind == "prep":
                            head = (0 if last else 2 * p + 2) if par else 2 * p + 1
                            prep(i, 1 - par, at, 2 * g + par + 1, head)
                        elif kind == "v":
                            v_group(i, at, g + 1)
                        elif kind == "maxrow":
                            max_row(at, 16 * (2 * g + par + 1))
                        elif kind == "sqrt":
                            sqrt(MISC_AT[last][("groupvar", 0)] + mb + 1, b + 1)
                    if t and t % KT == 0:
                        save_o(t // KT - 1, g)
                save_o(FINS - 1, g)

            def projection(b):
                act.wait_ge(added[0], PRIMED + FINS * ADDS * PAIRS * (b + 1))
                act.wait_ge(added[1], PRIMED + FINS * ADDS * PAIRS * (b + 1))
                act.wait_ge(misc_full, misc_base(b + 1, 0))
                act.wait_ge(res_coefs_ready, b + 1)
                for n in range(PJ):
                    act.wait_ge(proj_full, PJ * b + n + 1)
                    if n >= 8:
                        act.wait_ge(out_ready, PRIMED + PJ * b + n - 7)
                    a(proj_sb[:, n % 8, :], scores[:, n // 2 % 2, n % 2, 0:N], ACT.Identity,
                      bias=res_b[:, n % CT:n % CT + 1]).then_inc(proj_saved, 1)

            for s in (probs_ready, o_saved, proj_saved):
                act.sem_inc(s, PRIMED)
            sqrt(2, 0)
            act.wait_ge(consts_made, 8)
            for c in range(CH):
                prep(c, 0, 4 + c, 0, 0)
            for vg in range(VG):
                v_group(vg, 4 + CH + vg, 0)
            max_row(MISC_PRO, 0)
            with act.Fori(0, B) as b:
                for i in range(2):
                    act.wait_ge(stored[i], PRIMED + 16 * (CH // 2) * b)
                with act.Fori(0, PAIRS - 1) as p:
                    pair(b, p, False)
                pair(b, PAIRS - 1, True)
                projection(b)

        @block.vector
        def _(dve):
            v = nc.vector
            NORM_LINKS = CT + 7

            def low_parts(c, buf, misc_n):
                cs = slice(c * N, (c + 1) * N)
                dve.wait_ge(misc_free, misc_n)
                v.tensor_tensor(q_lo_max[buf][0:D, cs], qk_full[:, 0, :], q_hi_hi[buf][0:D, cs].bitcast(fp32),
                                ALU.subtract)
                v.tensor_tensor(k_hi_lo[buf][D:2 * D, cs], qk_full[:, 1, :], k_hi_lo[buf][0:D, cs].bitcast(fp32),
                                ALU.subtract).then_inc(lo_ready, 1)

            def unit_max(u, n, heads_done):
                dve.wait_ge(aux_full, n + 1)
                if u == 0:
                    dve.wait_ge(neg_ready, heads_done)
                v.tensor_reduce(maxima[:, u:u + 1], aux[:, :, 0:N], AX.XY, ALU.max).then_inc(max_done, 1)

            def negate_max(heads_done, misc_n):
                dve.wait_ge(max_done, UNITS * (heads_done + 1))
                dve.wait_ge(misc_full, misc_n)
                v.tensor_reduce(neg_max[:, :], maxima[:, :].rearrange("p (q c) -> p q c", c=BLOCKS), AX.X,
                                ALU.max, negate=True).then_inc(neg_ready, 1)

            def take_stats(i, k):
                dve.wait_ge(x_in, 16 * (2 * CT * k + i + 1))
                dve.wait_ge(stats_done, CT * k + i)
                for c in range(CH):
                    last = v.bn_stats(stats[:, c, :], xtile[:, c * N:(c + 1) * N])
                last.then_inc(chain, 1)
                dve.wait_ge(chain, NORM_LINKS * k + i + 1)
                v.memset(spare[:, :], 0.0)
                v.bn_aggr(meanvar[:, i, :], stats[:, :, :]).then_inc(stats_done, 1)

            def link(ins, n):
                ins.then_inc(chain, 1)
                dve.wait_ge(chain, n)

            def deviations(k, misc_n):
                at = NORM_LINKS * k + CT
                dve.wait_ge(misc_full, misc_n)
                dve.wait_ge(coefs_ready, k)
                v.tensor_tensor(dev, meanvar[:, :, 0], misc[:, 0:CT], ALU.subtract)
                v.tensor_copy(gmean, misc[:, 0:CT]).then_inc(misc_free, 1)
                dve.wait_ge(misc_free, misc_n)
                link(v.tensor_tensor(inv, dev, dev, ALU.mult), at + 1)
                v.tensor_tensor(tmp, inv, meanvar[:, :, 1], ALU.add).then_inc(dev_ready, 1)

            def group_variance(misc_n):
                dve.wait_ge(misc_full, misc_n)
                v.tensor_scalar_add(gvar, misc[:, 0:CT], EPS).then_inc(misc_free, 1)

            def coefs(k):
                at = NORM_LINKS * k + CT + 1
                dve.wait_ge(root_ready, k + 1)
                dve.wait_ge(dev_ready, k + 1)
                link(v.reciprocal(inv, root), at + 1)
                link(v.tensor_tensor(tmp, inv, inv, ALU.mult), at + 2)
                link(v.tensor_tensor(tmp, tmp, gvar, ALU.mult), at + 3)
                link(v.tensor_scalar(tmp, tmp, -0.5, 1.5, ALU.mult, ALU.add), at + 4)
                link(v.tensor_tensor(inv, inv, tmp, ALU.mult), at + 5)
                dve.wait_ge(res_coefs_ready, k)
                v.tensor_tensor(next_a, inv, gw, ALU.mult).then_inc(chain, 1)
                dve.wait_ge(chain, at + 6)
                v.tensor_tensor(tmp, gmean, next_a, ALU.mult).then_inc(shift_ready, 1)
                dve.wait_ge(shift_ready, k + 1)
                v.tensor_tensor(next_b, gb, tmp, ALU.subtract).then_inc(coefs_ready, 1)

            def normalize(i, k):
                dve.wait_ge(coefs_ready, k + 1)
                dve.wait_ge(x_in, 16 * (2 * CT * k + CT + i + 1))
                v.tensor_scalar(xn[:, i, :], xtile[:, :], next_a[:, i:i + 1], next_b[:, i:i + 1],
                                ALU.mult, ALU.add).then_inc(xn_ready, 1)

            def add(t, g):
                kt = t % KT
                if kt % 2 or kt == 0:
                    return
                j = t // KT
                dve.wait_ge(probs_ready, PRIMED + PSTEPS * g + t + 1)
                acc = denom[:, j % 2, 0, :]
                now = probs[:, t % RING * QB:(t % RING + 1) * QB]
                if kt == 2:
                    first = probs[:, (t - 2) % RING * QB:((t - 2) % RING + 1) * QB]
                    v.tensor_tensor(acc, first, now, ALU.add).then_inc(added[0], 1)
                else:
                    dve.wait_ge(added[0], PRIMED + FINS * ADDS * g + j * ADDS + kt // 2 - 1)
                    v.tensor_tensor(acc, acc, now, ALU.add).then_inc(added[0], 1)

            def finish(j, g, misc_n, stores):
                dve.wait_ge(misc_full, misc_n)
                dve.wait_ge(o_normed, PRIMED + FINS * g + j)
                v.reciprocal(recip[:, :], misc[:, 0:N]).then_inc(misc_free, 1)
                dve.wait_ge(misc_free, misc_n)
                dve.wait_ge(o_saved, PRIMED + FINS * g + j + 1)
                dve.wait_ge(att_out, PRIMED + stores)
                v.tensor_tensor(o_norm[:, :], o_raw[:, :], recip[:, :], ALU.mult).then_inc(o_normed, 1)

            def pair(b, p, last):
                g = pair_no(b, p)
                before, after = PLANS[last]
                mb = misc_base(b, p)
                for t in range(PSTEPS):
                    par = t // STEPS
                    done = 2 * g + par + 1
                    for kind, i in before[t]:
                        if kind == "aux":
                            unit_max(i, UNITS * done + i, done)
                        elif kind == "maxrow":
                            negate_max(done, mb)
                    add(t, g)
                    for kind, i in before[t]:
                        at = MISC_AT[last].get(key(par, kind, i), 0) + mb + 1
                        if kind == "prep":
                            low_parts(i, 1 - par, at)
                        elif kind == "finish":
                            finish(i, g, at, 32 * (FINS * g + i))
                        elif kind == "stats":
                            take_stats(i, b + 1)
                        elif kind == "groupmean":
                            deviations(b + 1, at)
                        elif kind == "groupvar":
                            group_variance(at)
                        elif kind == "coefs":
                            coefs(b + 1)
                        elif kind == "normalize":
                            if i == 0:
                                dve.wait_ge(misc_full, mb + MISC_AT[last][(0, "prep", CH - 1)] + 1)
                            normalize(i, b + 1)
                    for _, i in after[t]:
                        unit_max(i, UNITS * done + i, done)
                finish(FINS - 1, g, mb + MISC_AT[last][("finish", FINS - 1)] + 1, 32 * (FINS * g + FINS - 1))

            def projection(b):
                for n in range(PJ):
                    tc, ot = n // CT, n % CT
                    i = tc % 2
                    if ot == 0:
                        dve.wait_ge(xres_in[i], 16 * (CH // 2 * b + tc // 2 + 1))
                    dve.wait_ge(proj_saved, PRIMED + PJ * b + n + 1)
                    tile = xres(i)[:, ot, :]
                    v.scalar_tensor_tensor(tile, tile, res_a[:, ot:ot + 1], proj_sb[:, n % 8, :],
                                           ALU.mult, ALU.add).then_inc(out_ready, 1)

            for s in (added[0], o_normed, out_ready):
                dve.sem_inc(s, PRIMED)
            v.memset(ones[:, :], 1.0).then_inc(consts_made, 1)
            for i in range(2):
                v.memset(k_hi_one[i][D:D + 1, :].bitcast(fp32), 1.0).then_inc(consts_made, 1)
            dve.wait_ge(consts_in, 80)
            for i in range(CT):
                take_stats(i, 0)
            deviations(0, 1)
            group_variance(2)
            v.tensor_scalar(bqk_s[:, :], bqk_s[:, :], QK_SCALE, None, ALU.mult).then_inc(consts_made, 1)
            coefs(0)
            for i in range(CT):
                normalize(i, 0)
            dve.wait_ge(misc_full, 3)
            v.tensor_tensor(pb, pb, misc[:, 0:CT], ALU.add).then_inc(misc_free, 1)
            for c in range(CH):
                low_parts(c, 0, 4 + c)
            for u in range(UNITS):
                unit_max(u, u, 0)
            negate_max(0, 1)
            with dve.Fori(0, B) as b:
                dve.wait_ge(coefs_ready, b + 1)
                dve.wait_ge(out_ready, PRIMED + PJ * b)
                dve.wait_ge(proj_saved, PRIMED + PJ * b)
                dve.wait_ge(misc_free, 3)
                v.tensor_copy(res_a, next_a)
                v.tensor_tensor(res_b, next_b, pb, ALU.add).then_inc(res_coefs_ready, 1)
                with dve.Fori(0, PAIRS - 1) as p:
                    pair(b, p, False)
                pair(b, PAIRS - 1, True)
                projection(b)

        @block.gpsimd
        def _(pool):
            gp = nc.gpsimd

            def add(t, g):
                kt = t % KT
                if kt % 2 == 0 or kt == 1:
                    return
                j = t // KT
                pool.wait_ge(probs_ready, PRIMED + PSTEPS * g + t + 1)
                acc = denom[:, j % 2, 1, :]
                now = probs[:, t % RING * QB:(t % RING + 1) * QB]
                if kt == 3:
                    first = probs[:, (t - 2) % RING * QB:((t - 2) % RING + 1) * QB]
                    if j >= 2:
                        pool.wait_ge(o_normed, PRIMED + FINS * g + j - 1)
                    gp.tensor_tensor(acc, first, now, ALU.add).then_inc(added[1], 1)
                else:
                    pool.wait_ge(added[1], PRIMED + FINS * ADDS * g + j * ADDS + kt // 2 - 1)
                    gp.tensor_tensor(acc, acc, now, ALU.add).then_inc(added[1], 1)

            def pair(b, p, last):
                g = pair_no(b, p)
                pool.wait_ge(out_ready, PRIMED + PJ * b)
                pool.wait_ge(o_normed, PRIMED + FINS * g)
                for t in range(PSTEPS):
                    add(t, g)

            pool.sem_inc(added[1], PRIMED)
            gp.memset(ident[:, :], 0.0).then_inc(masks_filled, 1)
            gp.memset(groups[:, :], 1.0 / GROUP).then_inc(masks_filled, 1)
            pool.wait_ge(masks_filled, 2)
            gp.affine_select(out=ident[:, :], in_=ident[:, :], compare_op=ALU.not_equal, fill=1.0,
                             base=0, pattern=[[-1, 128]], channel_multiplier=1).then_inc(consts_made, 2)
            gv = groups[:, :].rearrange("p (g c) -> p g c", c=GROUP)
            gp.affine_select(out=gv, in_=gv, compare_op=ALU.is_ge, fill=0.0, base=0,
                             pattern=[[-GROUP, 128 // GROUP], [0, GROUP]], channel_multiplier=1)\
              .then_inc(masks_filled, 1)
            pool.wait_ge(masks_filled, 3)
            gp.affine_select(out=gv, in_=gv, compare_op=ALU.is_ge, fill=0.0, base=GROUP - 1,
                             pattern=[[GROUP, 128 // GROUP], [0, GROUP]], channel_multiplier=-1)\
              .then_inc(consts_made, 2)
            with pool.Fori(0, B) as b:
                with pool.Fori(0, PAIRS - 1) as p:
                    pair(b, p, False)
                pair(b, PAIRS - 1, True)


def kernel(**inputs):
    import numpy as np
    import concourse.bacc as bacc
    from concourse import mybir
    from concourse.bass_utils import run_bass_kernel_spmd

    x = np.asarray(inputs["x"])
    B, C, HH, WW = x.shape
    H, CT = 8, C // 128
    D = C // H
    bqkv = np.asarray(inputs["L0_conv_qkv_b"]).reshape(H, 3 * D)

    def columns(v):
        return np.ascontiguousarray(np.asarray(v).reshape(CT, 128).T)

    arrays = {
        "x": np.ascontiguousarray(x.reshape(B, C, HH * WW)),
        "gn_w": columns(inputs["L0_conv_gn_w"]),
        "gn_b": columns(inputs["L0_conv_gn_b"]),
        "wqkv_t": np.ascontiguousarray(np.asarray(inputs["L0_conv_qkv_w"]).T).reshape(C, H, 3 * D),
        "bqk": np.ascontiguousarray(bqkv[:, :2 * D].T),
        "bv": columns(bqkv[:, 2 * D:]),
        "wproj_t": np.ascontiguousarray(np.asarray(inputs["L0_conv_proj_w"]).T),
        "bproj": columns(inputs["L0_conv_proj_b"]),
    }
    nc = bacc.Bacc("TRN2", target_bir_lowering=False, num_devices=1)
    fp32 = mybir.dt.float32
    aps = {n: nc.dram_tensor(n, v.shape, mybir.dt.from_np(v.dtype), kind="ExternalInput").ap()
           for n, v in arrays.items()}
    att = nc.dram_tensor("att", (CT, 128, HH * WW), fp32, kind="Internal").ap()
    out = nc.dram_tensor("out", (B, C, HH * WW), fp32, kind="ExternalOutput").ap()
    attention_block_program(nc, att=att, out=out, **aps)
    r = run_bass_kernel_spmd(nc, [arrays], core_ids=[0])
    return r.results[0]["out"].reshape(B, C, HH, WW)
```

```python
import concourse.bass as bass
from concourse import mybir
from contextlib import ExitStack


def attention_block_program(nc, x, gn_w, gn_b, wqkv_t, bqk, bv, wproj_t, bproj, att, out):
    fp32 = mybir.dt.float32
    fp32r = mybir.dt.float32r
    ALU = mybir.AluOpType
    ACT = mybir.ActivationFunctionType
    AX = mybir.AxisListType

    B, C, T = x.shape
    H = 8
    D = C // H
    CT = C // 128
    GROUP = C // 32
    EPS = 1e-5
    QK_SCALE = float(D) ** -0.25
    PAIRS = H // 2
    N = 384
    QB = 2 * N
    BLOCKS = T // QB
    KT = T // 128
    CH = T // N
    STEPS = BLOCKS * KT
    PSTEPS = 2 * STEPS
    UNITS = KT * CH
    AUX_FIRST, AUX_LAST = 8, 47
    PIECES = 4
    VG = KT // 3
    RING = 4
    BY_VECTOR = ((0, 1, 3, 5, 7, 12, 17), (0, 1, 9, 17), (0, 1, 9, 13, 15, 17))
    ADDED = tuple((tiles, tuple(kt for kt in range(KT) if kt not in tiles)) for tiles in BY_VECTOR)
    ADDS = tuple(tuple(len(tiles[e]) - 1 for tiles in ADDED) for e in range(2))
    FINS = 2 * BLOCKS
    PRIMED = 1
    PJ = CH * CT

    def plan(last):
        within, before, after = ([[] for _ in range(PSTEPS)] for _ in range(3))
        for par in range(2):
            t0 = par * STEPS
            for c in range(CH):
                before[t0 + 1 + c].append(("prep", c))
            for j in range(BLOCKS):
                t = t0 + (j + 1) * KT + 2
                if t < PSTEPS:
                    before[t].append(("finish", par * BLOCKS + j))
                    if j < BLOCKS - 1:
                        for i in range(PIECES):
                            before[t + 1 + i].append(("recip", (par * BLOCKS + j, i)))
            room = [(s, slot) for s in range(AUX_FIRST, AUX_LAST + 1) for slot in (within, before, after)
                    if slot is not after or not any(k == "recip" for k, _ in before[t0 + s])]
            for u in range(UNITS):
                s, slot = room[u * len(room) // UNITS]
                slot[t0 + s].append(("aux", u))
            before[t0 + AUX_LAST + 2].append(("maxrow", 0))
        for g, t in enumerate((49, 50, 51, 52, 53, 53)):
            before[STEPS + t].append(("v", g))
        if last:
            for i in range(CT):
                before[10 + 6 * i].append(("stats", i))
                before[40 + 3 * i].append(("normalize", i))
            before[33].append(("groupmean", 0))
            before[35].append(("groupvar", 0))
            before[36].append(("sqrt", 0))
            before[37].append(("coefs", 0))
        return within, before, after

    PLANS = {last: plan(last) for last in (False, True)}
    BANKS = 3
    POOLED = ("prep", "v", "aux", "maxrow", "finish", "groupmean", "groupvar")
    TAIL = ("finish", FINS - 1)

    def use_key(par, kind, i):
        return (par, kind, i) if kind in ("prep", "aux", "maxrow") else (kind, i)

    def deal(keys):
        return {k: (n % BANKS, n // BANKS) for n, k in enumerate(keys)}

    def pair_uses(last):
        within, before, after = PLANS[last]
        keys = [use_key(t // STEPS, kind, i) for t in range(PSTEPS)
                for kind, i in within[t] + before[t] + after[t] if kind in POOLED]
        return deal(keys + [TAIL])

    def first_uses():
        keys = [("groupmean", 0), ("groupvar", 0), ("bias", 0)] + [("prep", c) for c in range(CH)]
        for u in range(UNITS):
            keys.append(("aux", u))
            if u % (UNITS // VG) == UNITS // VG // 2:
                keys.append(("v", u // (UNITS // VG)))
        return deal(keys + [("maxrow", 0)])

    USES = {last: pair_uses(last) for last in (False, True)}
    FIRST_USES = first_uses()

    def uses_in(table, bank):
        return sum(1 for k, _ in table.values() if k == bank)

    def uses_before(bank, b, p):
        pair, last = uses_in(USES[False], bank), uses_in(USES[True], bank)
        return uses_in(FIRST_USES, bank) + b * ((PAIRS - 1) * pair + last) + p * pair

    def use(last, b, p, key):
        bank, n = USES[last][key]
        return bank, uses_before(bank, b, p) + n

    with ExitStack() as ctx:
        def sb(name, shape, dt=fp32):
            return ctx.enter_context(nc.sbuf_tensor(name, shape, dt))

        def sem(name):
            return ctx.enter_context(nc.semaphore(name))

        q_hi_hi = [sb(f"q_hi_hi{i}", [128, T], fp32r) for i in range(2)]
        q_lo_max = [sb(f"q_lo_max{i}", [D + 1, T], fp32r) for i in range(2)]
        k_hi_lo = [sb(f"k_hi_lo{i}", [128, T], fp32r) for i in range(2)]
        k_hi_one = [sb(f"k_hi_one{i}", [D + 1, T], fp32r) for i in range(2)]
        xn = sb("xn", [128, CT, T])
        xtile = sb("xtile", [128, T])
        v_even = sb("v_even", [128, KT, D])
        v_odd = sb("v_odd", [128, KT, D])
        v_odd_next = sb("v_odd_next", [128, KT, D])
        probs = sb("probs", [128, RING * QB])
        denom = sb("denom", [128, 2, 2, QB])
        qk_full = sb("qk_full", [D, 2, N])
        o_raw = sb("o_raw", [128, N])
        sums = sb("sums", [128, N])
        recip = sb("recip", [128, N])
        o_norm = sb("o_norm", [128, N])
        wqk = [sb(f"wqk{i}", [128, CT, 128]) for i in range(2)]
        wv = sb("wv", [128, CT, 128])
        wproj = sb("wproj", [128, CT, C])
        att_in = [sb(f"att_in{i}", [128, CT, N]) for i in range(2)]
        ident = sb("ident", [128, 128])
        groups = sb("groups", [128, 128])
        ones = sb("ones", [128, D])
        maxima = sb("maxima", [128, UNITS])
        neg_max = sb("neg_max", [128, KT])
        max_rows = sb("max_rows", [KT, 128], fp32r)
        bqk_s = sb("bqk_s", [128, H])
        spare = sb("spare", [128, 1])
        head_bias = sb("head_bias", [128, 1])
        small = sb("small", [128, 64])
        stats = sb("stats", [128, CH, 6])

        def cols(n):
            return small[:, CT * n:CT * (n + 1)]

        gw, gb, pb, bvs = cols(0), cols(1), cols(2), cols(3)
        next_a, next_b, res_a, res_b = cols(4), cols(5), cols(6), cols(7)
        dev, gmean, tmp, gvar, root, inv = cols(8), cols(9), cols(10), cols(11), cols(12), cols(13)
        meanvar = sb("meanvar", [128, CT, 2])

        def xres(i):
            return probs[:, 2 * QB * i:2 * QB * (i + 1)].rearrange("p (o n) -> p o n", n=N)

        proj_sb = denom[:, :, :, :].rearrange("p a e (h n) -> p (a e h) n", n=N)

        scores = ctx.enter_context(nc.psum_tensor("scores", [128, 2, 2, 512], fp32))
        oacc = ctx.enter_context(nc.psum_tensor("oacc", [128, 512], fp32))
        pool_banks = ctx.enter_context(nc.psum_tensor("pool_banks", [128, BANKS, 512], fp32))

        consts_in = sem("consts_in")
        wproj_in = sem("wproj_in")
        wqk_in = [sem(f"wqk_in{i}") for i in range(2)]
        wv_in = sem("wv_in")
        x_in = sem("x_in")
        x0_in = [sem(f"x0_in{i}") for i in range(CT)]
        consts_made = sem("consts_made")
        stats_done = sem("stats_done")
        dev_ready = sem("dev_ready")
        root_ready = sem("root_ready")
        coefs_ready = sem("coefs_ready")
        xn_ready = sem("xn_ready")
        chain = sem("chain")
        shift_ready = sem("shift_ready")
        masks_filled = sem("masks_filled")
        res_coefs_ready = sem("res_coefs_ready")
        bank_full = [sem(f"bank_full{i}") for i in range(BANKS)]
        bank_free = [sem(f"bank_free{i}") for i in range(BANKS)]
        hi_ready = sem("hi_ready")
        lo_ready = sem("lo_ready")
        copies_ready = sem("copies_ready")
        bias_ready = sem("bias_ready")
        neg_ready = sem("neg_ready")
        maxrow_in = sem("maxrow_in")
        v_odd_ready = sem("v_odd_ready")
        scores_full = sem("scores_full")
        probs_ready = sem("probs_ready")
        pv_done = sem("pv_done")
        added = [sem("added_dve"), sem("added_pool")]
        o_saved = sem("o_saved")
        recip_ready = sem("recip_ready")
        o_normed = sem("o_normed")
        att_out = sem("att_out")
        att_back = [sem(f"att_back{i}") for i in range(2)]
        xres_in = [sem(f"xres_in{i}") for i in range(2)]
        proj_full = sem("proj_full")
        proj_saved = sem("proj_saved")
        out_ready = sem("out_ready")
        stored = [sem(f"stored{i}") for i in range(2)]

        block = ctx.enter_context(nc.Block())

        def first_batch(k):
            return isinstance(k, int)

        def adder(t):
            return 0 if t % KT in ADDED[t // KT % BLOCKS][0] else 1

        def adds_before(e, j):
            return sum(ADDS[e]) * (j // BLOCKS) + sum(ADDS[e][:j % BLOCKS])

        def adds_in_pairs(e, g):
            return 2 * sum(ADDS[e]) * g

        def adds_by(t):
            e, j = adder(t), t // KT
            return adds_before(e, j) + max(1, ADDED[j % BLOCKS][e].index(t % KT))

        def wait_full(engine, u):
            engine.wait_ge(bank_full[u[0]], u[1] + 1)

        def wait_free(engine, u):
            engine.wait_ge(bank_free[u[0]], u[1] + 1)

        def pair_no(b, p):
            return b * PAIRS + p

        @block.sync
        def _(sp):
            def load_wqk(h, buf):
                src = wqkv_t.rearrange("(k c) h n -> c k h n", c=128)[:, :, bass.ds(h, 1), 0:2 * D]
                sp.dma_start(wqk[buf][:, :, :], src.rearrange("c k h n -> c k (h n)")).then_inc(wqk_in[buf], 16)

            def load_wv(p):
                for i in range(2):
                    src = wqkv_t.rearrange("(k c) h n -> c k h n", c=128)[:, :, bass.ds(2 * p + i, 1), 2 * D:3 * D]
                    sp.dma_start(wv[:, :, i * D:(i + 1) * D],
                                 src.rearrange("c k h n -> c k (h n)")).then_inc(wv_in, 16)

            def load_x(b, i):
                sp.dma_start(xtile[:, :], x[bass.ds(b, 1), i * 128:(i + 1) * 128, :]
                             .rearrange("b c t -> (b c) t")).then_inc(x_in, 16)

            def copy_chunk(c, buf, n):
                cs = slice(c * N, (c + 1) * N)
                sp.wait_ge(hi_ready, n)
                sp.dma_start(q_hi_hi[buf][D:2 * D, cs].bitcast(fp32),
                             q_hi_hi[buf][0:D, cs].bitcast(fp32)).then_inc(copies_ready, 16)
                sp.dma_start(k_hi_one[buf][0:D, cs].bitcast(fp32),
                             k_hi_lo[buf][0:D, cs].bitcast(fp32)).then_inc(copies_ready, 16)

            def put_max_row(buf, u):
                wait_free(sp, u)
                sp.dma_start(q_lo_max[buf][D:D + 1, :].bitcast(fp32).rearrange("o (t q) -> o t q", q=128),
                             max_rows[:, :].bitcast(fp32)).then_inc(maxrow_in, 16)

            def norm_load(b, i, k, second):
                if second:
                    if i:
                        sp.wait_ge(xn_ready, CT * k + i)
                    else:
                        sp.wait_ge(stats_done, CT * (k + 1))
                elif i:
                    sp.wait_ge(stats_done, CT * k + i)
                load_x(b, i)

            def put_block(b, p, j, g):
                par, blk = j // BLOCKS, j % BLOCKS
                sp.wait_ge(o_normed, PRIMED + FINS * g + j + 1)
                for half in range(2):
                    q0 = blk * QB + half * N
                    dst = att[bass.ds(p, 1), par * D:(par + 1) * D, q0:q0 + N].rearrange("a c t -> (a c) t")
                    sp.dma_start(dst, o_norm[half * D:(half + 1) * D, :]).then_inc(att_out, 16)

            def pair(b, p, last):
                g = pair_no(b, p)
                _, before, _ = PLANS[last]
                nb = (b + 1) % B
                if last:
                    sp.wait_ge(xn_ready, CT * (b + 1))
                    norm_load(nb, 0, b + 1, False)
                for t in range(PSTEPS):
                    par = t // STEPS
                    if t % STEPS == 10:
                        if par == 0:
                            wait_full(sp, use(last, b, p, (0, "prep", CH - 1)))
                            load_wqk(0 if last else 2 * p + 2, 0)
                            load_wv(0 if last else p + 1)
                        else:
                            wait_full(sp, use(last, b, p, (1, "prep", CH - 1)))
                            load_wqk(1 if last else 2 * p + 3, 1)
                    for kind, i in before[t]:
                        if kind == "prep":
                            copy_chunk(i, 1 - par, CH * (2 * g + par + 1) + i + 1)
                        elif kind == "maxrow":
                            put_max_row(1 - par, use(last, b, p, (par, kind, i)))
                        elif kind == "finish":
                            put_block(b, p, i, g)
                        elif kind == "stats" and i + 1 < CT:
                            norm_load(nb, i + 1, b + 1, False)
                        elif kind == "coefs":
                            norm_load(nb, 0, b + 1, True)
                        elif kind == "normalize" and i + 1 < CT:
                            norm_load(nb, i + 1, b + 1, True)
                if not last:
                    put_block(b, p, FINS - 1, g)

            def load_att(b, tc):
                i = tc % 2
                sp.dma_start(att_in[i][:, :, :], att[:, :, tc * N:(tc + 1) * N]
                             .rearrange("k c t -> c k t")).then_inc(att_back[i], 16)

            def chan(ap, b, tc):
                return ap[bass.ds(b, 1), :, tc * N:(tc + 1) * N].rearrange("b (k c) t -> c (b k) t", c=128)

            def projection(b):
                g = pair_no(b, PAIRS - 1)
                puts = 32 * FINS
                sp.wait_ge(att_out, PRIMED + puts * g + 32 * (FINS - 1))
                load_att(b, 0)
                load_att(b, 1)
                put_block(b, PAIRS - 1, FINS - 1, g)
                for tc in range(2):
                    sp.dma_start(xres(tc), chan(x, b, tc)).then_inc(xres_in[tc], 16)
                for tc in range(CH):
                    i = tc % 2
                    sp.wait_ge(out_ready, PRIMED + PJ * b + CT * (tc + 1))
                    sp.dma_start(chan(out, b, tc), xres(i)).then_inc(stored[i], 16)
                    if tc + 2 < CH:
                        if tc + 2 == 2 * (CH // 3):
                            sp.wait_ge(att_out, PRIMED + puts * (g + 1))
                        load_att(b, tc + 2)
                        sp.wait_ge(stored[i], PRIMED + 16 * (CH // 2 * b + tc // 2 + 1))
                        sp.dma_start(xres(i), chan(x, b, tc + 2)).then_inc(xres_in[i], 16)

            for s in (att_out, stored[0], stored[1]):
                sp.sem_inc(s, PRIMED)
            for i in range(CT):
                sp.dma_start(xn[:, i, :], x[0, i * 128:(i + 1) * 128, :]).then_inc(x0_in[i], 16)
            load_wqk(0, 0)
            for dst, src in ((gw, gn_w), (gb, gn_b), (pb, bproj), (bvs, bv), (bqk_s[:, :], bqk)):
                sp.dma_start(dst, src).then_inc(consts_in, 16)
            sp.dma_start(wproj[:, :, :], wproj_t.rearrange("(k c) n -> c k n", c=128)).then_inc(wproj_in, 16)
            load_wqk(1, 1)
            load_wv(0)
            for c in range(CH):
                copy_chunk(c, 0, c + 1)
            put_max_row(0, FIRST_USES["maxrow", 0])
            with sp.Fori(0, B) as b:
                with sp.Fori(0, PAIRS - 1) as p:
                    pair(b, p, False)
                pair(b, PAIRS - 1, True)
                projection(b)
            for i in range(2):
                sp.wait_ge(stored[i], PRIMED + 16 * (CH // 2) * B)
            sp.wait_ge(att_out, PRIMED + 32 * FINS * PAIRS * B)
            sp.wait_ge(maxrow_in, 16 * (H * B + 1))
            for i in range(2):
                sp.wait_ge(wqk_in[i], 16 * (PAIRS * B + 1))
            sp.wait_ge(wv_in, 32 * (PAIRS * B + 1))

        @block.tensor
        def _(pe):
            mm = nc.tensor.matmul

            def bank_for(u):
                if not isinstance(u[1], int) or u[1] > 0:
                    pe.wait_ge(bank_free[u[0]], u[1])
                return pool_banks[:, u[0]]

            def filled(ins, u):
                ins.then_inc(bank_full[u[0]], 1)

            def prep(c, buf, u, wait_w):
                if c == 0:
                    pe.wait_ge(wqk_in[buf], wait_w)
                bank = bank_for(u)
                for k in range(CT):
                    last = mm(bank[:, 0:N], wqk[buf][:, k, :], xn[:, k, c * N:(c + 1) * N],
                              start=(k == 0), stop=(k == CT - 1))
                filled(last, u)

            def v_group(vg, u, wait_w):
                if vg == 0:
                    pe.wait_ge(wv_in, wait_w)
                bank = bank_for(u)
                for i in range(3):
                    tt = 3 * vg + i
                    for k in range(CT):
                        last = mm(bank[:, i * 128:(i + 1) * 128], xn[:, k, tt * 128:(tt + 1) * 128],
                                  wv[:, k, :], start=(k == 0), stop=(k == CT - 1))
                filled(last, u)

            def aux_unit(n, buf, head, u):
                qt, kc = n // CH, n % CH
                if n == 0:
                    pe.wait_ge(copies_ready, 32 * CH * (head + 1))
                    pe.wait_ge(lo_ready, CH * (head + 1))
                filled(mm(bank_for(u)[:, 0:N], q_hi_hi[buf][:, qt * 128:(qt + 1) * 128],
                          k_hi_lo[buf][:, kc * N:(kc + 1) * N], start=True, stop=True), u)

            def max_row(n, u):
                pe.wait_ge(neg_ready, n)
                filled(nc.tensor.transpose(bank_for(u)[0:KT, 0:128], neg_max[:, :], ident[:, :]), u)

            def group_mean(k, u):
                pe.wait_ge(stats_done, CT * (k + 1))
                filled(mm(bank_for(u)[:, 0:CT], groups[:, :], meanvar[:, :, 0], start=True, stop=True), u)

            def group_var(k, u):
                pe.wait_ge(dev_ready, k + 1)
                filled(mm(bank_for(u)[:, 0:CT], groups[:, :], tmp, start=True, stop=True), u)

            def finish(j, g, u):
                for e in range(2):
                    pe.wait_ge(added[e], PRIMED + adds_in_pairs(e, g) + adds_before(e, j + 1))
                bank = bank_for(u)
                for e in range(2):
                    for half in range(2):
                        last = mm(bank[half * D:(half + 1) * D, 0:N], ones[:, :],
                                  denom[:, j % 2, e, half * N:(half + 1) * N], start=(e == 0), stop=(e == 1))
                filled(last, u)

            def make_scores(t, g, part):
                par, s = t // STEPS, t % STEPS
                blk, kt = s // KT, s % KT
                if part == 0:
                    pe.wait_ge(probs_ready, PRIMED + PSTEPS * g + max(0, t - 1))
                elif s == 0:
                    pe.wait_ge(maxrow_in, 16 * (2 * g + par + 1))
                kk, qq = ((k_hi_lo, q_hi_hi), (k_hi_one, q_lo_max))[part]
                for half in range(2):
                    q0 = blk * QB + half * N
                    last = mm(scores[:, t % 2, half, 0:N], kk[par][:, kt * 128:(kt + 1) * 128],
                              qq[par][:, q0:q0 + N], start=(part == 0), stop=(part == 1))
                if part == 1:
                    last.then_inc(scores_full, 1)

            def make_pv(t, b, p):
                g = pair_no(b, p)
                par, s = t // STEPS, t % STEPS
                kt = s % KT
                if t == 0:
                    for k in range(BANKS):
                        pe.wait_ge(bank_free[k], uses_before(k, b, p))
                if t == STEPS:
                    pe.wait_ge(v_odd_ready, g + 1)
                pe.wait_ge(probs_ready, PRIMED + PSTEPS * g + t + 1)
                if kt == 0:
                    pe.wait_ge(o_saved, PRIMED + FINS * g + t // KT)
                v = v_odd if par else v_even
                p0 = t % RING * QB
                for half in range(2):
                    last = mm(oacc[half * D:(half + 1) * D, 0:N], v[:, kt, :],
                              probs[:, p0 + half * N:p0 + (half + 1) * N], start=(kt == 0), stop=(kt == KT - 1))
                last.then_inc(pv_done, 1)

            def pair(b, p, last):
                g = pair_no(b, p)
                within, before, after = PLANS[last]
                pe.wait_ge(proj_saved, PRIMED + PJ * b)
                for t in range(PSTEPS):
                    par = t // STEPS
                    make_scores(t, g, 0)
                    for kind, i in within[t]:
                        behind(t, kind, i, b, p, last)
                    make_scores(t, g, 1)
                    for kind, i in before[t]:
                        behind(t, kind, i, b, p, last)
                    if t:
                        make_pv(t - 1, b, p)
                    for kind, i in after[t]:
                        behind(t, kind, i, b, p, last)
                make_pv(PSTEPS - 1, b, p)
                finish(FINS - 1, g, use(last, b, p, TAIL))

            def behind(t, kind, i, b, p, last):
                par, g = t // STEPS, pair_no(b, p)
                if kind not in POOLED:
                    return
                u = use(last, b, p, use_key(par, kind, i))
                if kind == "prep":
                    if last and par == 1 and i == 0:
                        pe.wait_ge(xn_ready, CT * (b + 2))
                    prep(i, 1 - par, u, 16 * (g + 2 if par else g + 1))
                elif kind == "v":
                    v_group(i, u, 32 * (g + 2))
                elif kind == "aux":
                    aux_unit(i, 1 - par, 2 * g + par + 1, u)
                elif kind == "maxrow":
                    max_row(2 * g + par + 2, u)
                elif kind == "finish":
                    finish(i, g, u)
                elif kind == "groupmean":
                    group_mean(b + 1, u)
                else:
                    group_var(b + 1, u)

            def projection(b):
                for tc in range(CH):
                    i = tc % 2
                    pe.wait_ge(att_back[i], 16 * (CH // 2 * b + tc // 2 + 1))
                    for ot in range(CT):
                        n = tc * CT + ot
                        if n >= 4:
                            pe.wait_ge(proj_saved, PRIMED + PJ * b + n - 3)
                        for k in range(CT):
                            last = mm(scores[:, n // 2 % 2, n % 2, 0:N], wproj[:, k, ot * 128:(ot + 1) * 128],
                                      att_in[i][:, k, :], start=(k == 0), stop=(k == CT - 1))
                        last.then_inc(proj_full, 1)

            pe.sem_inc(pv_done, PRIMED)
            pe.wait_ge(consts_made, 7)
            group_mean(0, FIRST_USES["groupmean", 0])
            group_var(0, FIRST_USES["groupvar", 0])
            pe.wait_ge(wproj_in, 16)
            pe.wait_ge(consts_in, 80)
            bank = bank_for(FIRST_USES["bias", 0])
            for ot in range(CT):
                for k in range(CT):
                    last = mm(bank[:, ot:ot + 1], wproj[:, k, ot * 128:(ot + 1) * 128], bvs[:, k:k + 1],
                              start=(k == 0), stop=(k == CT - 1))
            filled(last, FIRST_USES["bias", 0])
            pe.wait_ge(xn_ready, CT)
            for key, u in FIRST_USES.items():
                kind, i = key
                if kind == "prep":
                    prep(i, 0, u, 16)
                elif kind == "v":
                    v_group(i, u, 32)
                elif kind == "aux":
                    aux_unit(i, 0, 0, u)
                elif kind == "maxrow":
                    max_row(1, u)
            with pe.Fori(0, B) as b:
                with pe.Fori(0, PAIRS - 1) as p:
                    pair(b, p, False)
                pair(b, PAIRS - 1, True)
                projection(b)

        @block.scalar
        def _(act):
            a = nc.scalar.activation

            def prep(c, buf, u, heads, head):
                cs = slice(c * N, (c + 1) * N)
                bq, bk = head_bias[0:D, :], head_bias[D:2 * D, :]
                if c == 0:
                    a(head_bias[:, :], bqk_s[:, bass.ds(head, 1)], ACT.Copy).then_inc(bias_ready, 1)
                    act.wait_ge(bias_ready, heads + 1)
                wait_full(act, u)
                bank = pool_banks[:, u[0]]
                a(q_hi_hi[buf][0:D, cs], bank[0:D, 0:N], ACT.Identity, scale=QK_SCALE, bias=bq)
                a(k_hi_lo[buf][0:D, cs], bank[D:2 * D, 0:N], ACT.Identity, scale=QK_SCALE,
                  bias=bk).then_inc(hi_ready, 1)
                act.wait_ge(lo_ready, CH * heads + c)
                a(qk_full[:, 0, :], bank[0:D, 0:N], ACT.Identity, scale=QK_SCALE, bias=bq)
                a(qk_full[:, 1, :], bank[D:2 * D, 0:N], ACT.Identity, scale=QK_SCALE,
                  bias=bk).then_inc(bank_free[u[0]], 1)

            def v_group(vg, u, copied):
                wait_full(act, u)
                if vg == 0 and copied is not None:
                    act.wait_ge(v_odd_ready, copied)
                m = pool_banks[:, u[0], 0:3 * 128].rearrange("p (t h c) -> p h t c", t=3, h=2)
                a(v_odd_next[:, 3 * vg:3 * vg + 3, :], m[:, 1], ACT.Copy)
                a(v_even[:, 3 * vg:3 * vg + 3, :], m[:, 0], ACT.Copy).then_inc(bank_free[u[0]], 1)

            def max_row(u, rows_sent):
                wait_full(act, u)
                if rows_sent is not None:
                    act.wait_ge(maxrow_in, rows_sent)
                a(max_rows[:, :], pool_banks[0:KT, u[0], 0:128], ACT.Copy).then_inc(bank_free[u[0]], 1)

            def save_sums(j, g, u):
                wait_full(act, u)
                act.wait_ge(o_normed, PRIMED + FINS * g + j)
                a(sums[:, :], pool_banks[:, u[0], 0:N], ACT.Copy).then_inc(bank_free[u[0]], 1)

            def sqrt(u):
                wait_free(act, u)
                a(root, gvar, ACT.Sqrt).then_inc(root_ready, 1)

            def save_o(j, g):
                act.wait_ge(pv_done, PRIMED + PSTEPS * g + KT * (j + 1))
                act.wait_ge(o_normed, PRIMED + FINS * g + j)
                a(o_raw[:, :], oacc[:, 0:N], ACT.Copy).then_inc(o_saved, 1)

            def pair(b, p, last):
                g = pair_no(b, p)
                _, before, _ = PLANS[last]
                for t in range(PSTEPS):
                    par = t // STEPS
                    act.wait_ge(pv_done, PRIMED + PSTEPS * g + max(0, t - RING + 1))
                    if t < RING:
                        if t == 0:
                            for e in range(2):
                                act.wait_ge(added[e], PRIMED + adds_in_pairs(e, g))
                    else:
                        e = adder(t - RING)
                        act.wait_ge(added[e], PRIMED + adds_in_pairs(e, g) + adds_by(t - RING))
                    act.wait_ge(scores_full, PSTEPS * g + t + 1)
                    a(probs[:, t % RING * QB:(t % RING + 1) * QB].rearrange("p (h n) -> p h n", n=N),
                      scores[:, t % 2, :, 0:N], ACT.Exp).then_inc(probs_ready, 1)
                    if t == 3:
                        for k in range(BANKS):
                            act.wait_ge(bank_free[k], uses_before(k, b, p))
                        a(v_odd[:, :, :], v_odd_next[:, :, :], ACT.Copy).then_inc(v_odd_ready, 1)
                    for kind, i in before[t]:
                        u = use(last, b, p, use_key(par, kind, i)) if kind in POOLED else None
                        if kind == "prep":
                            head = (0 if last else 2 * p + 2) if par else 2 * p + 1
                            prep(i, 1 - par, u, 2 * g + par + 1, head)
                        elif kind == "v":
                            v_group(i, u, g + 1)
                        elif kind == "maxrow":
                            max_row(u, 16 * (2 * g + par + 1))
                        elif kind == "finish":
                            save_sums(i, g, u)
                        elif kind == "sqrt":
                            sqrt(use(last, b, p, ("groupvar", 0)))
                    if t and t % KT == 0:
                        save_o(t // KT - 1, g)
                save_o(FINS - 1, g)
                save_sums(FINS - 1, g, use(last, b, p, TAIL))

            def projection(b):
                act.wait_ge(res_coefs_ready, b + 1)
                for n in range(PJ):
                    act.wait_ge(proj_full, PJ * b + n + 1)
                    if n >= 8:
                        act.wait_ge(out_ready, PRIMED + PJ * b + n - 7)
                    a(proj_sb[:, n % 8, :], scores[:, n // 2 % 2, n % 2, 0:N], ACT.Identity,
                      bias=res_b[:, n % CT:n % CT + 1]).then_inc(proj_saved, 1)

            for s in (probs_ready, o_saved, proj_saved):
                act.sem_inc(s, PRIMED)
            sqrt(FIRST_USES["groupvar", 0])
            act.wait_ge(consts_made, 8)
            for (kind, i), u in FIRST_USES.items():
                if kind == "prep":
                    prep(i, 0, u, 0, 0)
                elif kind == "v":
                    v_group(i, u, None)
                elif kind == "maxrow":
                    max_row(u, None)
            with act.Fori(0, B) as b:
                for i in range(2):
                    act.wait_ge(stored[i], PRIMED + 16 * (CH // 2) * b)
                with act.Fori(0, PAIRS - 1) as p:
                    pair(b, p, False)
                pair(b, PAIRS - 1, True)
                projection(b)

        @block.vector
        def _(dve):
            v = nc.vector
            NORM_LINKS = CT + 7

            def low_parts(c, buf, u):
                cs = slice(c * N, (c + 1) * N)
                wait_free(dve, u)
                v.tensor_tensor(q_lo_max[buf][0:D, cs], qk_full[:, 0, :], q_hi_hi[buf][0:D, cs].bitcast(fp32),
                                ALU.subtract)
                v.tensor_tensor(k_hi_lo[buf][D:2 * D, cs], qk_full[:, 1, :], k_hi_lo[buf][0:D, cs].bitcast(fp32),
                                ALU.subtract).then_inc(lo_ready, 1)

            def unit_max(n, u, heads_done):
                wait_full(dve, u)
                if n == 0 and heads_done is not None:
                    dve.wait_ge(neg_ready, heads_done)
                v.tensor_reduce(maxima[:, n:n + 1], pool_banks[:, u[0], 0:N], AX.X, ALU.max)\
                 .then_inc(bank_free[u[0]], 1)

            def negate_max(last_unit, last_row):
                wait_free(dve, last_unit)
                if last_row is not None:
                    wait_full(dve, last_row)
                v.tensor_reduce(neg_max[:, :], maxima[:, :].rearrange("p (q c) -> p q c", c=CH), AX.X,
                                ALU.max, negate=True).then_inc(neg_ready, 1)

            def take_stats(i, k):
                tile = xtile[:, :]
                if first_batch(k):
                    tile = xn[:, i, :]
                    dve.wait_ge(x0_in[i], 16)
                else:
                    dve.wait_ge(x_in, 16 * (2 * CT * (k - 1) + i + 1))
                if i or not first_batch(k):
                    dve.wait_ge(stats_done, CT * k + i)
                for c in range(CH):
                    last = v.bn_stats(stats[:, c, :], tile[:, c * N:(c + 1) * N])
                last.then_inc(chain, 1)
                dve.wait_ge(chain, NORM_LINKS * k + i + 1)
                v.memset(spare[:, :], 0.0)
                v.bn_aggr(meanvar[:, i, :], stats[:, :, :]).then_inc(stats_done, 1)

            def link(ins, n):
                ins.then_inc(chain, 1)
                dve.wait_ge(chain, n)

            def deviations(k, u):
                at = NORM_LINKS * k + CT
                wait_full(dve, u)
                if not first_batch(k):
                    dve.wait_ge(coefs_ready, k)
                v.tensor_tensor(dev, meanvar[:, :, 0], pool_banks[:, u[0], 0:CT], ALU.subtract)
                v.tensor_copy(gmean, pool_banks[:, u[0], 0:CT]).then_inc(bank_free[u[0]], 1)
                wait_free(dve, u)
                link(v.tensor_tensor(inv, dev, dev, ALU.mult), at + 1)
                v.tensor_tensor(tmp, inv, meanvar[:, :, 1], ALU.add).then_inc(dev_ready, 1)

            def group_variance(u):
                wait_full(dve, u)
                v.tensor_scalar_add(gvar, pool_banks[:, u[0], 0:CT], EPS).then_inc(bank_free[u[0]], 1)

            def coefs(k):
                at = NORM_LINKS * k + CT + 1
                dve.wait_ge(root_ready, k + 1)
                dve.wait_ge(dev_ready, k + 1)
                link(v.reciprocal(inv, root), at + 1)
                link(v.tensor_tensor(tmp, inv, inv, ALU.mult), at + 2)
                link(v.tensor_tensor(tmp, tmp, gvar, ALU.mult), at + 3)
                link(v.tensor_scalar(tmp, tmp, -0.5, 1.5, ALU.mult, ALU.add), at + 4)
                link(v.tensor_tensor(inv, inv, tmp, ALU.mult), at + 5)
                if not first_batch(k):
                    dve.wait_ge(res_coefs_ready, k)
                v.tensor_tensor(next_a, inv, gw, ALU.mult).then_inc(chain, 1)
                dve.wait_ge(chain, at + 6)
                v.tensor_tensor(tmp, gmean, next_a, ALU.mult).then_inc(shift_ready, 1)
                dve.wait_ge(shift_ready, k + 1)
                v.tensor_tensor(next_b, gb, tmp, ALU.subtract).then_inc(coefs_ready, 1)

            def normalize(i, k):
                dve.wait_ge(coefs_ready, k + 1)
                tile = xn[:, i, :]
                if not first_batch(k):
                    tile = xtile[:, :]
                    dve.wait_ge(x_in, 16 * (2 * CT * (k - 1) + CT + i + 1))
                v.tensor_scalar(xn[:, i, :], tile, next_a[:, i:i + 1], next_b[:, i:i + 1],
                                ALU.mult, ALU.add).then_inc(xn_ready, 1)

            def add(t, g):
                kt, j = t % KT, t // KT
                tiles = ADDED[j % BLOCKS][0]
                if kt not in tiles[1:]:
                    return
                i = tiles.index(kt)
                dve.wait_ge(probs_ready, PRIMED + PSTEPS * g + t + 1)
                acc = denom[:, j % 2, 0, :]
                now = probs[:, t % RING * QB:(t % RING + 1) * QB]
                if i == 1:
                    t0 = t - kt + tiles[0]
                    first = probs[:, t0 % RING * QB:(t0 % RING + 1) * QB]
                    v.tensor_tensor(acc, first, now, ALU.add).then_inc(added[0], 1)
                else:
                    dve.wait_ge(added[0], PRIMED + adds_in_pairs(0, g) + adds_by(t) - 1)
                    v.tensor_tensor(acc, acc, now, ALU.add).then_inc(added[0], 1)

            def take_recip(j, g, u, pieces, of):
                for i in pieces:
                    cs = slice(i * N // of, (i + 1) * N // of)
                    if i == 0:
                        wait_free(dve, u)
                        dve.wait_ge(o_normed, PRIMED + FINS * g + j)
                    last = v.reciprocal(recip[:, cs], sums[:, cs])
                if i == of - 1:
                    last.then_inc(recip_ready, 1)
                    dve.wait_ge(recip_ready, FINS * g + j + 1)
                    dve.wait_ge(o_saved, PRIMED + FINS * g + j + 1)
                    dve.wait_ge(att_out, PRIMED + 32 * (FINS * g + j))
                    v.tensor_tensor(o_norm[:, :], o_raw[:, :], recip[:, :], ALU.mult).then_inc(o_normed, 1)

            def pair(b, p, last):
                g = pair_no(b, p)
                within, before, after = PLANS[last]
                for t in range(PSTEPS):
                    par = t // STEPS
                    done = 2 * g + par + 1
                    for kind, i in within[t] + before[t]:
                        if kind == "aux":
                            unit_max(i, use(last, b, p, (par, kind, i)), done)
                        elif kind == "maxrow":
                            negate_max(use(last, b, p, (par, "aux", UNITS - 1)),
                                       use(last, b, p, (0, "maxrow", 0)) if par else None)
                    add(t, g)
                    for kind, i in before[t]:
                        u = use(last, b, p, use_key(par, kind, i)) if kind in POOLED else None
                        if kind == "prep":
                            low_parts(i, 1 - par, u)
                        elif kind == "finish" and i % BLOCKS == BLOCKS - 1:
                            take_recip(i, g, u, (0,), 1)
                        elif kind == "recip":
                            j, piece = i
                            take_recip(j, g, use(last, b, p, ("finish", j)), (piece,), PIECES)
                        elif kind == "stats":
                            take_stats(i, b + 1)
                        elif kind == "groupmean":
                            deviations(b + 1, u)
                        elif kind == "groupvar":
                            group_variance(u)
                        elif kind == "coefs":
                            coefs(b + 1)
                        elif kind == "normalize":
                            if i == 0:
                                wait_full(dve, use(last, b, p, (0, "prep", CH - 1)))
                            normalize(i, b + 1)
                    for _, i in after[t]:
                        unit_max(i, use(last, b, p, (par, "aux", i)), done)
                take_recip(FINS - 1, g, use(last, b, p, TAIL), (0,), 1)

            def projection(b):
                for n in range(PJ):
                    tc, ot = n // CT, n % CT
                    i = tc % 2
                    if ot == 0:
                        dve.wait_ge(xres_in[i], 16 * (CH // 2 * b + tc // 2 + 1))
                    dve.wait_ge(proj_saved, PRIMED + PJ * b + n + 1)
                    tile = xres(i)[:, ot, :]
                    v.scalar_tensor_tensor(tile, tile, res_a[:, ot:ot + 1], proj_sb[:, n % 8, :],
                                           ALU.mult, ALU.add).then_inc(out_ready, 1)

            for s in (added[0], o_normed, out_ready):
                dve.sem_inc(s, PRIMED)
            v.memset(ones[:, :], 1.0).then_inc(consts_made, 1)
            for i in range(2):
                v.memset(k_hi_one[i][D:D + 1, :].bitcast(fp32), 1.0).then_inc(consts_made, 1)
            dve.wait_ge(consts_in, 80)
            for i in range(CT):
                take_stats(i, 0)
            deviations(0, FIRST_USES["groupmean", 0])
            group_variance(FIRST_USES["groupvar", 0])
            v.tensor_scalar(bqk_s[:, :], bqk_s[:, :], QK_SCALE, None, ALU.mult).then_inc(consts_made, 1)
            coefs(0)
            for i in range(CT):
                normalize(i, 0)
            u = FIRST_USES["bias", 0]
            wait_full(dve, u)
            v.tensor_tensor(pb, pb, pool_banks[:, u[0], 0:CT], ALU.add).then_inc(bank_free[u[0]], 1)
            for (kind, i), u in FIRST_USES.items():
                if kind == "prep":
                    low_parts(i, 0, u)
                elif kind == "aux":
                    unit_max(i, u, None)
            negate_max(FIRST_USES["aux", UNITS - 1], None)
            with dve.Fori(0, B) as b:
                dve.wait_ge(coefs_ready, b + 1)
                dve.wait_ge(out_ready, PRIMED + PJ * b)
                dve.wait_ge(proj_saved, PRIMED + PJ * b)
                wait_free(dve, FIRST_USES["bias", 0])
                v.tensor_copy(res_a, next_a)
                v.tensor_tensor(res_b, next_b, pb, ALU.add).then_inc(res_coefs_ready, 1)
                with dve.Fori(0, PAIRS - 1) as p:
                    pair(b, p, False)
                pair(b, PAIRS - 1, True)
                projection(b)

        @block.gpsimd
        def _(pool):
            gp = nc.gpsimd

            def add(t, g):
                kt, j = t % KT, t // KT
                tiles = ADDED[j % BLOCKS][1]
                if kt not in tiles[1:]:
                    return
                i = tiles.index(kt)
                pool.wait_ge(probs_ready, PRIMED + PSTEPS * g + t + 1)
                acc = denom[:, j % 2, 1, :]
                now = probs[:, t % RING * QB:(t % RING + 1) * QB]
                if i == 1:
                    t0 = t - kt + tiles[0]
                    first = probs[:, t0 % RING * QB:(t0 % RING + 1) * QB]
                    if j >= 2:
                        pool.wait_ge(o_normed, PRIMED + FINS * g + j - 1)
                    gp.tensor_tensor(acc, first, now, ALU.add).then_inc(added[1], 1)
                else:
                    pool.wait_ge(added[1], PRIMED + adds_in_pairs(1, g) + adds_by(t) - 1)
                    gp.tensor_tensor(acc, acc, now, ALU.add).then_inc(added[1], 1)

            def pair(b, p, last):
                g = pair_no(b, p)
                pool.wait_ge(out_ready, PRIMED + PJ * b)
                pool.wait_ge(o_normed, PRIMED + FINS * g)
                for t in range(PSTEPS):
                    add(t, g)

            pool.sem_inc(added[1], PRIMED)
            gp.memset(ident[:, :], 0.0).then_inc(masks_filled, 1)
            gp.memset(groups[:, :], 1.0 / GROUP).then_inc(masks_filled, 1)
            pool.wait_ge(masks_filled, 2)
            gp.affine_select(out=ident[:, :], in_=ident[:, :], compare_op=ALU.not_equal, fill=1.0,
                             base=0, pattern=[[-1, 128]], channel_multiplier=1).then_inc(consts_made, 2)
            gv = groups[:, :].rearrange("p (g c) -> p g c", c=GROUP)
            gp.affine_select(out=gv, in_=gv, compare_op=ALU.is_ge, fill=0.0, base=0,
                             pattern=[[-GROUP, 128 // GROUP], [0, GROUP]], channel_multiplier=1)\
              .then_inc(masks_filled, 1)
            pool.wait_ge(masks_filled, 3)
            gp.affine_select(out=gv, in_=gv, compare_op=ALU.is_ge, fill=0.0, base=GROUP - 1,
                             pattern=[[GROUP, 128 // GROUP], [0, GROUP]], channel_multiplier=-1)\
              .then_inc(consts_made, 2)
            with pool.Fori(0, B) as b:
                with pool.Fori(0, PAIRS - 1) as p:
                    pair(b, p, False)
                pair(b, PAIRS - 1, True)


def kernel(**inputs):
    import numpy as np
    import concourse.bacc as bacc
    from concourse import mybir
    from concourse.bass_utils import run_bass_kernel_spmd

    x = np.asarray(inputs["x"])
    B, C, HH, WW = x.shape
    H, CT = 8, C // 128
    D = C // H
    bqkv = np.asarray(inputs["L0_conv_qkv_b"]).reshape(H, 3 * D)

    def columns(v):
        return np.ascontiguousarray(np.asarray(v).reshape(CT, 128).T)

    arrays = {
        "x": np.ascontiguousarray(x.reshape(B, C, HH * WW)),
        "gn_w": columns(inputs["L0_conv_gn_w"]),
        "gn_b": columns(inputs["L0_conv_gn_b"]),
        "wqkv_t": np.ascontiguousarray(np.asarray(inputs["L0_conv_qkv_w"]).T).reshape(C, H, 3 * D),
        "bqk": np.ascontiguousarray(bqkv[:, :2 * D].T),
        "bv": columns(bqkv[:, 2 * D:]),
        "wproj_t": np.ascontiguousarray(np.asarray(inputs["L0_conv_proj_w"]).T),
        "bproj": columns(inputs["L0_conv_proj_b"]),
    }
    nc = bacc.Bacc("TRN2", target_bir_lowering=False, num_devices=1)
    fp32 = mybir.dt.float32
    aps = {n: nc.dram_tensor(n, v.shape, mybir.dt.from_np(v.dtype), kind="ExternalInput").ap()
           for n, v in arrays.items()}
    att = nc.dram_tensor("att", (CT, 128, HH * WW), fp32, kind="Internal").ap()
    out = nc.dram_tensor("out", (B, C, HH * WW), fp32, kind="ExternalOutput").ap()
    attention_block_program(nc, att=att, out=out, **aps)
    r = run_bass_kernel_spmd(nc, [arrays], core_ids=[0])
    return r.results[0]["out"].reshape(B, C, HH, WW)
```

```python
import concourse.bass as bass
from concourse import mybir
from contextlib import ExitStack


def attention_block_program(nc, x, gn_w, gn_b, wqkv_t, bqk, bv, wproj_t, bproj, att, out):
    fp32 = mybir.dt.float32
    fp32r = mybir.dt.float32r
    ALU = mybir.AluOpType
    ACT = mybir.ActivationFunctionType
    AX = mybir.AxisListType

    B, C, T = x.shape
    H = 8
    D = C // H
    CT = C // 128
    GROUP = C // 32
    EPS = 1e-5
    QK_SCALE = float(D) ** -0.25
    PAIRS = H // 2
    N = 384
    QB = 2 * N
    BLOCKS = T // QB
    KT = T // 128
    CH = T // N
    STEPS = BLOCKS * KT
    PSTEPS = 2 * STEPS
    UNITS = KT * CH
    AUX_FIRST, AUX_LAST = 8, 47
    STATS_AT = 1
    NORM_AT, NORM_STEPS = 18, 7
    PIECES = 4
    VG = KT // 3
    RING = 4
    BY_VECTOR = ((0, 1, 3, 5, 7, 12, 17), (0, 1, 9, 17), (0, 1, 9, 13, 15, 17))
    ADDED = tuple((tiles, tuple(kt for kt in range(KT) if kt not in tiles)) for tiles in BY_VECTOR)
    ADDS = tuple(tuple(len(tiles[e]) - 1 for tiles in ADDED) for e in range(2))
    FINS = 2 * BLOCKS
    PRIMED = 1
    PJ = CH * CT

    INNER, LAST, END = range(3)

    def plan(kind_of_pair):
        within, before, after = ([[] for _ in range(PSTEPS)] for _ in range(3))
        for par in range(2):
            t0 = par * STEPS
            more = not (kind_of_pair == END and par == 1)
            for c in range(CH if more else 0):
                before[t0 + 1 + c].append(("prep", c))
            for j in range(BLOCKS):
                t = t0 + (j + 1) * KT + (2 if j == BLOCKS - 1 else 3)
                if t < PSTEPS:
                    before[t].append(("finish", par * BLOCKS + j))
                    if j < BLOCKS - 1:
                        for i in range(PIECES):
                            before[t + 1 + i].append(("recip", (par * BLOCKS + j, i)))
            room = [(s, slot) for s in range(AUX_FIRST, AUX_LAST + 1) for slot in (within, before, after)
                    if slot is not after or not any(k == "recip" for k, _ in before[t0 + s])]
            for u in range(UNITS if more else 0):
                s, slot = room[u * len(room) // UNITS]
                slot[t0 + s].append(("aux", u))
            if more:
                before[t0 + AUX_LAST + 2].append(("maxrow", 0))
        if kind_of_pair != END:
            for g, t in enumerate((49, 50, 51, 52, 53, 53)):
                before[STEPS + t].append(("v", g))
        if kind_of_pair == LAST:
            for i in range(CT):
                for part in range(BLOCKS):
                    before[STATS_AT + (BLOCKS * i + part) // 2].append(("stats", (i, part)))
                    before[NORM_AT + NORM_STEPS * i + part].append(("normalize", (i, part)))
            before[10].append(("groupmean", 0))
            before[12].append(("groupvar", 0))
            before[13].append(("sqrt", 0))
            before[14].append(("coefs", 0))
        return within, before, after

    PLANS = [plan(kind) for kind in (INNER, LAST, END)]
    BANKS = 3
    FIRST_VG = UNITS // (VG - 2)
    POOLED = ("prep", "v", "aux", "maxrow", "finish", "groupmean", "groupvar")
    TAIL = ("finish", FINS - 1)

    def use_key(par, kind, i):
        return (par, kind, i) if kind in ("prep", "aux", "maxrow") else (kind, i)

    def deal(keys):
        return {k: (n % BANKS, n // BANKS) for n, k in enumerate(keys)}

    def pair_uses(kind_of_pair):
        within, before, after = PLANS[kind_of_pair]
        keys = [use_key(t // STEPS, kind, i) for t in range(PSTEPS)
                for kind, i in within[t] + before[t] + after[t] if kind in POOLED]
        return deal(keys + [TAIL])

    def first_units(c):
        return [u for u in range(UNITS) if max(u // CH * 128 // N, u % CH) == c]

    def first_uses():
        keys = [("groupmean", 0), ("groupvar", 0), ("bias", 0), ("prep", 0)]
        units = 0
        for c in range(CH):
            if c + 1 < CH:
                keys.append(("prep", c + 1))
            for u in first_units(c):
                keys.append(("aux", u))
                units += 1
                if units % FIRST_VG == FIRST_VG // 2 and units // FIRST_VG < VG - 2:
                    keys.append(("v", units // FIRST_VG))
        return deal(keys + [("v", VG - 2), ("maxrow", 0), ("v", VG - 1)])

    USES = [pair_uses(kind) for kind in (INNER, LAST, END)]
    FIRST_USES = first_uses()

    def uses_in(table, bank):
        return sum(1 for k, _ in table.values() if k == bank)

    def uses_before(bank, b, p):
        pair, last = uses_in(USES[INNER], bank), uses_in(USES[LAST], bank)
        return uses_in(FIRST_USES, bank) + b * ((PAIRS - 1) * pair + last) + p * pair

    def use(kp, b, p, key):
        bank, n = USES[kp][key]
        return bank, uses_before(bank, b, p) + n

    with ExitStack() as ctx:
        def sb(name, shape, dt=fp32):
            return ctx.enter_context(nc.sbuf_tensor(name, shape, dt))

        def sem(name):
            return ctx.enter_context(nc.semaphore(name))

        q_hi_hi = [sb(f"q_hi_hi{i}", [128, T], fp32r) for i in range(2)]
        q_lo_max = [sb(f"q_lo_max{i}", [D + 1, T], fp32r) for i in range(2)]
        k_hi_lo = [sb(f"k_hi_lo{i}", [128, T], fp32r) for i in range(2)]
        k_hi_one = [sb(f"k_hi_one{i}", [D + 1, T], fp32r) for i in range(2)]
        xn = sb("xn", [128, CT, T])
        xtile = sb("xtile", [128, T])
        v_even = sb("v_even", [128, KT, D])
        v_odd = sb("v_odd", [128, KT, D])
        v_odd_next = sb("v_odd_next", [128, KT, D])
        probs = sb("probs", [128, RING * QB])
        denom = sb("denom", [128, 2, 2, QB])
        qk_full = sb("qk_full", [D, 2, N])
        o_raw = sb("o_raw", [128, N])
        sums = sb("sums", [128, N])
        recip = sb("recip", [128, N])
        o_norm = sb("o_norm", [128, N])
        wqk = [sb(f"wqk{i}", [128, CT, 128]) for i in range(2)]
        wv = sb("wv", [128, CT, 128])
        wproj_hi = sb("wproj_hi", [128, CT, C], fp32r)
        wproj_lo = sb("wproj_lo", [128, CT, C], fp32r)
        att_in = [sb(f"att_in{i}", [128, CT, N], fp32r) for i in range(2)]
        ident = sb("ident", [128, 128])
        groups = sb("groups", [128, 128])
        ones = sb("ones", [128, D])
        maxima = sb("maxima", [128, UNITS])
        neg_max = sb("neg_max", [128, KT])
        max_rows = sb("max_rows", [KT, 128], fp32r)
        bqk_s = sb("bqk_s", [128, H])
        spare = sb("spare", [128, 1])
        head_bias = sb("head_bias", [128, 1])
        small = sb("small", [128, 64])
        stats = sb("stats", [128, CH, 6])

        def cols(n):
            return small[:, CT * n:CT * (n + 1)]

        gw, gb, pb, bvs = cols(0), cols(1), cols(2), cols(3)
        next_a, next_b, res_a, res_b = cols(4), cols(5), cols(6), cols(7)
        dev, gmean, tmp, gvar, root, inv = cols(8), cols(9), cols(10), cols(11), cols(12), cols(13)
        meanvar = sb("meanvar", [128, CT, 2])

        def xres(i):
            return probs[:, 2 * QB * i:2 * QB * (i + 1)].rearrange("p (o n) -> p o n", n=N)

        proj_sb = denom[:, :, :, :].rearrange("p a e (h n) -> p (a e h) n", n=N)

        def chunk_of(buf):
            return buf[:, 0:CT * N].rearrange("p (k n) -> p k n", n=N)

        att_hi = [chunk_of(q_hi_hi[1]), chunk_of(k_hi_lo[1])]
        wproj_full = xtile[:, 0:CT * C].rearrange("p (k n) -> p k n", n=C)

        scores = ctx.enter_context(nc.psum_tensor("scores", [128, 2, 2, 512], fp32))
        oacc = ctx.enter_context(nc.psum_tensor("oacc", [128, 512], fp32))
        pool_banks = ctx.enter_context(nc.psum_tensor("pool_banks", [128, BANKS, 512], fp32))

        consts_in = sem("consts_in")
        wproj_in = sem("wproj_in")
        wproj_hi_ready = sem("wproj_hi_ready")
        wproj_lo_ready = sem("wproj_lo_ready")
        wqk_in = [sem(f"wqk_in{i}") for i in range(2)]
        wv_in = sem("wv_in")
        x_in = [sem(f"x_in{i}") for i in range(BLOCKS)]
        x0_in = [sem(f"x0_in{i}") for i in range(CT)]
        consts_made = sem("consts_made")
        stats_taken = sem("stats_taken")
        stats_done = sem("stats_done")
        dev_ready = sem("dev_ready")
        root_ready = sem("root_ready")
        coefs_ready = sem("coefs_ready")
        xn_ready = sem("xn_ready")
        chain = sem("chain")
        shift_ready = sem("shift_ready")
        masks_filled = sem("masks_filled")
        res_coefs_ready = sem("res_coefs_ready")
        bank_full = [sem(f"bank_full{i}") for i in range(BANKS)]
        bank_free = [sem(f"bank_free{i}") for i in range(BANKS)]
        hi_ready = sem("hi_ready")
        lo_ready = sem("lo_ready")
        q_copied = [sem(f"q_copied{i}") for i in range(CH)]
        k_copied = sem("k_copied")
        bias_ready = sem("bias_ready")
        neg_ready = sem("neg_ready")
        maxrow_in = sem("maxrow_in")
        v_odd_ready = sem("v_odd_ready")
        scores_full = sem("scores_full")
        probs_ready = sem("probs_ready")
        pv_done = sem("pv_done")
        added = [sem("added_dve"), sem("added_pool")]
        merged = sem("merged")
        o_saved = sem("o_saved")
        recip_ready = sem("recip_ready")
        o_normed = sem("o_normed")
        att_out = sem("att_out")
        att_back = [sem(f"att_back{i}") for i in range(2)]
        att_hi_ready = sem("att_hi_ready")
        att_lo_ready = sem("att_lo_ready")
        xres_in = [sem(f"xres_in{i}") for i in range(2)]
        proj_full = sem("proj_full")
        proj_saved = sem("proj_saved")
        out_ready = sem("out_ready")
        stored = [sem(f"stored{i}") for i in range(2)]

        block = ctx.enter_context(nc.Block())

        def first_batch(k):
            return isinstance(k, int)

        def adder(t):
            return 0 if t % KT in ADDED[t // KT % BLOCKS][0] else 1

        def adds_before(e, j):
            return sum(ADDS[e]) * (j // BLOCKS) + sum(ADDS[e][:j % BLOCKS])

        def adds_in_pairs(e, g):
            return 2 * sum(ADDS[e]) * g

        def adds_by(t):
            e, j = adder(t), t // KT
            return adds_before(e, j) + max(1, ADDED[j % BLOCKS][e].index(t % KT))

        def wait_full(engine, u):
            engine.wait_ge(bank_full[u[0]], u[1] + 1)

        def wait_free(engine, u):
            engine.wait_ge(bank_free[u[0]], u[1] + 1)

        def pair_no(b, p):
            return b * PAIRS + p

        @block.sync
        def _(sp):
            def load_wqk(h, buf):
                src = wqkv_t.rearrange("(k c) h n -> c k h n", c=128)[:, :, bass.ds(h, 1), 0:2 * D]
                sp.dma_start(wqk[buf][:, :, :], src.rearrange("c k h n -> c k (h n)")).then_inc(wqk_in[buf], 16)

            def load_wv(p):
                for i in range(2):
                    src = wqkv_t.rearrange("(k c) h n -> c k h n", c=128)[:, :, bass.ds(2 * p + i, 1), 2 * D:3 * D]
                    sp.dma_start(wv[:, :, i * D:(i + 1) * D],
                                 src.rearrange("c k h n -> c k (h n)")).then_inc(wv_in, 16)

            def load_x(b, i, part):
                cs = slice(part * QB, (part + 1) * QB)
                sp.dma_start(xtile[:, cs], x[bass.ds(b, 1), i * 128:(i + 1) * 128, cs]
                             .rearrange("b c t -> (b c) t")).then_inc(x_in[part], 16)

            def copy_chunk(c, buf, n):
                cs = slice(c * N, (c + 1) * N)
                sp.wait_ge(hi_ready, n)
                sp.dma_start(q_hi_hi[buf][D:2 * D, cs].bitcast(fp32),
                             q_hi_hi[buf][0:D, cs].bitcast(fp32)).then_inc(q_copied[c], 16)
                sp.dma_start(k_hi_one[buf][0:D, cs].bitcast(fp32),
                             k_hi_lo[buf][0:D, cs].bitcast(fp32)).then_inc(k_copied, 16)

            def put_max_row(buf, u):
                wait_free(sp, u)
                sp.dma_start(q_lo_max[buf][D:D + 1, :].bitcast(fp32).rearrange("o (t q) -> o t q", q=128),
                             max_rows[:, :].bitcast(fp32)).then_inc(maxrow_in, 16)

            def stats_load(b, i, part, k):
                if i:
                    sp.wait_ge(stats_taken, BLOCKS * (CT * k + i - 1) + part + 1)
                load_x(b, i, part)

            def norm_load(b, i, part, k):
                if i:
                    sp.wait_ge(xn_ready, BLOCKS * (CT * k + i - 1) + part + 1)
                else:
                    sp.wait_ge(stats_taken, BLOCKS * (CT * k + CT - 1) + part + 1)
                load_x(b, i, part)

            def put_block(b, p, j, g):
                par, blk = j // BLOCKS, j % BLOCKS
                sp.wait_ge(o_normed, PRIMED + FINS * g + j + 1)
                for half in range(2):
                    q0 = blk * QB + half * N
                    dst = att[bass.ds(p, 1), par * D:(par + 1) * D, q0:q0 + N].rearrange("a c t -> (a c) t")
                    sp.dma_start(dst, o_norm[half * D:(half + 1) * D, :]).then_inc(att_out, 16)

            def pair(b, p, kp):
                g = pair_no(b, p)
                _, before, _ = PLANS[kp]
                nb = (b + 1) % B
                if kp == LAST:
                    sp.wait_ge(xn_ready, BLOCKS * CT * (b + 1))
                    for part in range(BLOCKS):
                        stats_load(nb, 0, part, b + 1)
                for t in range(PSTEPS):
                    par = t // STEPS
                    if t % STEPS == 10 and kp != END:
                        if par == 0:
                            wait_full(sp, use(kp, b, p, (0, "prep", CH - 1)))
                            load_wqk(0 if kp == LAST else 2 * p + 2, 0)
                            load_wv(0 if kp == LAST else p + 1)
                        else:
                            wait_full(sp, use(kp, b, p, (1, "prep", CH - 1)))
                            load_wqk(1 if kp == LAST else 2 * p + 3, 1)
                    for kind, i in before[t]:
                        if kind == "prep":
                            copy_chunk(i, 1 - par, CH * (2 * g + par + 1) + i + 1)
                        elif kind == "maxrow":
                            put_max_row(1 - par, use(kp, b, p, (par, kind, i)))
                        elif kind == "finish":
                            put_block(b, p, i, g)
                        elif kind == "stats":
                            tile, part = i
                            if tile + 1 < CT:
                                stats_load(nb, tile + 1, part, b + 1)
                            else:
                                norm_load(nb, 0, part, b + 1)
                        elif kind == "normalize" and i[0] + 1 < CT:
                            norm_load(nb, i[0] + 1, i[1], b + 1)
                if kp == INNER:
                    put_block(b, p, FINS - 1, g)

            def load_att(b, tc):
                i = tc % 2
                sp.dma_start(att_in[i][:, :, :].bitcast(fp32), att[:, :, tc * N:(tc + 1) * N]
                             .rearrange("k c t -> c k t")).then_inc(att_back[i], 16)

            def chan(ap, b, tc):
                return ap[bass.ds(b, 1), :, tc * N:(tc + 1) * N].rearrange("b (k c) t -> c (b k) t", c=128)

            def projection(b):
                g = pair_no(b, PAIRS - 1)
                puts = 32 * FINS
                sp.wait_ge(att_out, PRIMED + puts * g + 32 * (FINS - 1))
                load_att(b, 0)
                load_att(b, 1)
                put_block(b, PAIRS - 1, FINS - 1, g)
                for tc in range(2):
                    if tc == 1:
                        sp.wait_ge(att_out, PRIMED + puts * (g + 1))
                    sp.dma_start(xres(tc), chan(x, b, tc)).then_inc(xres_in[tc], 16)
                for tc in range(CH):
                    i = tc % 2
                    if tc + 2 < CH:
                        sp.wait_ge(proj_full, PJ * b + CT * (tc + 1))
                        load_att(b, tc + 2)
                    sp.wait_ge(out_ready, PRIMED + PJ * b + CT * (tc + 1))
                    sp.dma_start(chan(out, b, tc), xres(i)).then_inc(stored[i], 16)
                    if tc + 2 < CH:
                        sp.wait_ge(stored[i], PRIMED + 16 * (CH // 2 * b + tc // 2 + 1))
                        sp.dma_start(xres(i), chan(x, b, tc + 2)).then_inc(xres_in[i], 16)

            for s in (att_out, stored[0], stored[1]):
                sp.sem_inc(s, PRIMED)
            for i in range(CT):
                sp.dma_start(xn[:, i, :], x[0, i * 128:(i + 1) * 128, :]).then_inc(x0_in[i], 16)
            load_wqk(0, 0)
            for dst, src in ((gw, gn_w), (gb, gn_b), (pb, bproj), (bvs, bv), (bqk_s[:, :], bqk)):
                sp.dma_start(dst, src).then_inc(consts_in, 16)
            sp.dma_start(wproj_full, wproj_t.rearrange("(k c) n -> c k n", c=128)).then_inc(wproj_in, 16)
            load_wqk(1, 1)
            load_wv(0)
            for c in range(CH):
                copy_chunk(c, 0, c + 1)
            sp.wait_ge(wproj_lo_ready, 1)
            put_max_row(0, FIRST_USES["maxrow", 0])

            def batch(b, last_kind):
                with sp.Fori(0, PAIRS - 1) as p:
                    pair(b, p, INNER)
                pair(b, PAIRS - 1, last_kind)
                projection(b)

            with sp.Fori(0, B - 1) as b:
                batch(b, LAST)
            batch(B - 1, END)
            for i in range(2):
                sp.wait_ge(stored[i], PRIMED + 16 * (CH // 2) * B)
            sp.wait_ge(att_out, PRIMED + 32 * FINS * PAIRS * B)
            sp.wait_ge(maxrow_in, 16 * H * B)
            for i in range(2):
                sp.wait_ge(wqk_in[i], 16 * PAIRS * B)
            sp.wait_ge(wv_in, 32 * PAIRS * B)

        @block.tensor
        def _(pe):
            mm = nc.tensor.matmul

            def bank_for(u):
                if not isinstance(u[1], int) or u[1] > 0:
                    pe.wait_ge(bank_free[u[0]], u[1])
                return pool_banks[:, u[0]]

            def filled(ins, u):
                ins.then_inc(bank_full[u[0]], 1)

            def prep(c, buf, u, wait_w):
                if c == 0:
                    pe.wait_ge(wqk_in[buf], wait_w)
                bank = bank_for(u)
                for k in range(CT):
                    last = mm(bank[:, 0:N], wqk[buf][:, k, :], xn[:, k, c * N:(c + 1) * N],
                              start=(k == 0), stop=(k == CT - 1))
                filled(last, u)

            def v_group(vg, u, wait_w):
                if vg == 0:
                    pe.wait_ge(wv_in, wait_w)
                bank = bank_for(u)
                for i in range(3):
                    tt = 3 * vg + i
                    for k in range(CT):
                        last = mm(bank[:, i * 128:(i + 1) * 128], xn[:, k, tt * 128:(tt + 1) * 128],
                                  wv[:, k, :], start=(k == 0), stop=(k == CT - 1))
                filled(last, u)

            def aux_unit(n, buf, head, u):
                qt, kc = n // CH, n % CH
                if head is None:
                    for c in range(CH):
                        if n == first_units(c)[0]:
                            pe.wait_ge(lo_ready, c + 1)
                            pe.wait_ge(q_copied[c], 16)
                else:
                    if qt == 0:
                        pe.wait_ge(lo_ready, CH * head + kc + 1)
                    if kc == 0 and qt % (N // 128) == 0:
                        pe.wait_ge(q_copied[qt * 128 // N], 16 * (head + 1))
                filled(mm(bank_for(u)[:, 0:N], q_hi_hi[buf][:, qt * 128:(qt + 1) * 128],
                          k_hi_lo[buf][:, kc * N:(kc + 1) * N], start=True, stop=True), u)

            def max_row(n, u):
                pe.wait_ge(neg_ready, n)
                filled(nc.tensor.transpose(bank_for(u)[0:KT, 0:128], neg_max[:, :], ident[:, :]), u)

            def group_mean(k, u):
                pe.wait_ge(stats_done, CT * (k + 1))
                filled(mm(bank_for(u)[:, 0:CT], groups[:, :], meanvar[:, :, 0], start=True, stop=True), u)

            def group_var(k, u):
                pe.wait_ge(dev_ready, k + 1)
                filled(mm(bank_for(u)[:, 0:CT], groups[:, :], tmp, start=True, stop=True), u)

            def finish(j, g, u):
                engines = (0, 1) if j == FINS - 1 else (1,)
                if j == FINS - 1:
                    for e in engines:
                        pe.wait_ge(added[e], PRIMED + adds_in_pairs(e, g) + adds_before(e, j + 1))
                else:
                    pe.wait_ge(merged, (FINS - 1) * g + j + 1)
                bank = bank_for(u)
                for e in engines:
                    for half in range(2):
                        last = mm(bank[half * D:(half + 1) * D, 0:N], ones[:, :],
                                  denom[:, j % 2, e, half * N:(half + 1) * N],
                                  start=(e == engines[0]), stop=(e == 1))
                filled(last, u)

            def make_scores(t, g, part):
                par, s = t // STEPS, t % STEPS
                blk, kt = s // KT, s % KT
                if part == 0:
                    pe.wait_ge(probs_ready, PRIMED + PSTEPS * g + max(0, t - 1))
                elif s == 0:
                    pe.wait_ge(maxrow_in, 16 * (2 * g + par + 1))
                    pe.wait_ge(k_copied, 16 * CH * (2 * g + par + 1))
                kk, qq = ((k_hi_lo, q_hi_hi), (k_hi_one, q_lo_max))[part]
                for half in range(2):
                    q0 = blk * QB + half * N
                    last = mm(scores[:, t % 2, half, 0:N], kk[par][:, kt * 128:(kt + 1) * 128],
                              qq[par][:, q0:q0 + N], start=(part == 0), stop=(part == 1))
                if part == 1:
                    last.then_inc(scores_full, 1)

            def make_pv(t, b, p):
                g = pair_no(b, p)
                par, s = t // STEPS, t % STEPS
                kt = s % KT
                if t == 0:
                    for k in range(BANKS):
                        pe.wait_ge(bank_free[k], uses_before(k, b, p))
                if t == STEPS:
                    pe.wait_ge(v_odd_ready, g + 1)
                pe.wait_ge(probs_ready, PRIMED + PSTEPS * g + t + 1)
                if kt == 0:
                    pe.wait_ge(o_saved, PRIMED + FINS * g + t // KT)
                v = v_odd if par else v_even
                p0 = t % RING * QB
                for half in range(2):
                    last = mm(oacc[half * D:(half + 1) * D, 0:N], v[:, kt, :],
                              probs[:, p0 + half * N:p0 + (half + 1) * N], start=(kt == 0), stop=(kt == KT - 1))
                last.then_inc(pv_done, 1)

            def pair(b, p, kp):
                g = pair_no(b, p)
                within, before, after = PLANS[kp]
                pe.wait_ge(proj_saved, PRIMED + PJ * b)
                for t in range(PSTEPS):
                    par = t // STEPS
                    make_scores(t, g, 0)
                    for kind, i in within[t]:
                        behind(t, kind, i, b, p, kp)
                    make_scores(t, g, 1)
                    for kind, i in before[t]:
                        behind(t, kind, i, b, p, kp)
                    if t:
                        make_pv(t - 1, b, p)
                    for kind, i in after[t]:
                        behind(t, kind, i, b, p, kp)
                make_pv(PSTEPS - 1, b, p)
                finish(FINS - 1, g, use(kp, b, p, TAIL))

            def behind(t, kind, i, b, p, kp):
                par, g = t // STEPS, pair_no(b, p)
                if kind not in POOLED:
                    return
                u = use(kp, b, p, use_key(par, kind, i))
                if kind == "prep":
                    if kp == LAST and par == 1 and i == 0:
                        pe.wait_ge(xn_ready, BLOCKS * CT * (b + 2))
                    prep(i, 1 - par, u, 16 * (g + 2 if par else g + 1))
                elif kind == "v":
                    v_group(i, u, 32 * (g + 2))
                elif kind == "aux":
                    aux_unit(i, 1 - par, 2 * g + par + 1, u)
                elif kind == "maxrow":
                    max_row(2 * g + par + 2, u)
                elif kind == "finish":
                    finish(i, g, u)
                elif kind == "groupmean":
                    group_mean(b + 1, u)
                else:
                    group_var(b + 1, u)

            def projection(b):
                pe.wait_ge(wproj_lo_ready, 1)
                for tc in range(CH):
                    i = tc % 2
                    for low in range(2):
                        pe.wait_ge(att_lo_ready if low else att_hi_ready, CH * b + tc + 1)
                        products = ([(wproj_hi, att_in[i])] if low
                                    else [(wproj_hi, att_hi[i]), (wproj_lo, att_hi[i])])
                        for ot in range(CT):
                            n = tc * CT + ot
                            if not low and n >= 4:
                                pe.wait_ge(proj_saved, PRIMED + PJ * b + n - 3)
                            for w, a in products:
                                for k in range(CT):
                                    last = mm(scores[:, n // 2 % 2, n % 2, 0:N], w[:, k, ot * 128:(ot + 1) * 128],
                                              a[:, k, :], start=(not low and w is wproj_hi and k == 0),
                                              stop=(low == 1 and k == CT - 1))
                            if low:
                                last.then_inc(proj_full, 1)

            pe.sem_inc(pv_done, PRIMED)
            pe.wait_ge(consts_made, 7)
            group_mean(0, FIRST_USES["groupmean", 0])
            group_var(0, FIRST_USES["groupvar", 0])
            pe.wait_ge(wproj_in, 16)
            pe.wait_ge(consts_in, 80)
            bank = bank_for(FIRST_USES["bias", 0])
            for ot in range(CT):
                for k in range(CT):
                    last = mm(bank[:, ot:ot + 1], wproj_full[:, k, ot * 128:(ot + 1) * 128], bvs[:, k:k + 1],
                              start=(k == 0), stop=(k == CT - 1))
            filled(last, FIRST_USES["bias", 0])
            for key, u in FIRST_USES.items():
                kind, i = key
                if kind == "prep":
                    if i % 2 == 0:
                        pe.wait_ge(xn_ready, CT * (i // 2 + 1))
                    prep(i, 0, u, 16)
                elif kind == "v":
                    v_group(i, u, 32)
                elif kind == "aux":
                    aux_unit(i, 0, None, u)
                elif kind == "maxrow":
                    max_row(1, u)

            def batch(b, last_kind):
                with pe.Fori(0, PAIRS - 1) as p:
                    pair(b, p, INNER)
                pair(b, PAIRS - 1, last_kind)
                projection(b)

            with pe.Fori(0, B - 1) as b:
                batch(b, LAST)
            batch(B - 1, END)

        @block.scalar
        def _(act):
            a = nc.scalar.activation

            def prep(c, buf, u, heads, head):
                cs = slice(c * N, (c + 1) * N)
                bq, bk = head_bias[0:D, :], head_bias[D:2 * D, :]
                if c == 0:
                    a(head_bias[:, :], bqk_s[:, bass.ds(head, 1)], ACT.Copy).then_inc(bias_ready, 1)
                    act.wait_ge(bias_ready, heads + 1)
                wait_full(act, u)
                bank = pool_banks[:, u[0]]
                a(q_hi_hi[buf][0:D, cs], bank[0:D, 0:N], ACT.Identity, scale=QK_SCALE, bias=bq)
                a(k_hi_lo[buf][0:D, cs], bank[D:2 * D, 0:N], ACT.Identity, scale=QK_SCALE,
                  bias=bk).then_inc(hi_ready, 1)
                act.wait_ge(lo_ready, CH * heads + c)
                a(qk_full[:, 0, :], bank[0:D, 0:N], ACT.Identity, scale=QK_SCALE, bias=bq)
                a(qk_full[:, 1, :], bank[D:2 * D, 0:N], ACT.Identity, scale=QK_SCALE,
                  bias=bk).then_inc(bank_free[u[0]], 1)

            def v_group(vg, u, copied):
                wait_full(act, u)
                if vg == 0 and copied is not None:
                    act.wait_ge(v_odd_ready, copied)
                m = pool_banks[:, u[0], 0:3 * 128].rearrange("p (t h c) -> p h t c", t=3, h=2)
                a(v_odd_next[:, 3 * vg:3 * vg + 3, :], m[:, 1], ACT.Copy)
                a(v_even[:, 3 * vg:3 * vg + 3, :], m[:, 0], ACT.Copy).then_inc(bank_free[u[0]], 1)

            def max_row(u, rows_sent):
                wait_full(act, u)
                if rows_sent is not None:
                    act.wait_ge(maxrow_in, rows_sent)
                a(max_rows[:, :], pool_banks[0:KT, u[0], 0:128], ACT.Copy).then_inc(bank_free[u[0]], 1)

            def save_sums(j, g, u):
                wait_full(act, u)
                act.wait_ge(o_normed, PRIMED + FINS * g + j)
                a(sums[:, :], pool_banks[:, u[0], 0:N], ACT.Copy).then_inc(bank_free[u[0]], 1)

            def sqrt(u):
                wait_free(act, u)
                a(root, gvar, ACT.Sqrt).then_inc(root_ready, 1)

            def normalize(i, part, k):
                cs = slice(part * QB, (part + 1) * QB)
                tile = xn[:, i, cs]
                if not first_batch(k):
                    tile = xtile[:, cs]
                    act.wait_ge(x_in[part], 16 * (2 * CT * (k - 1) + CT + i + 1))
                act.wait_ge(coefs_ready, k + 1)
                a(xn[:, i, cs], tile, ACT.Identity, scale=next_a[:, i:i + 1],
                  bias=next_b[:, i:i + 1]).then_inc(xn_ready, 1)

            def save_o(j, g):
                act.wait_ge(pv_done, PRIMED + PSTEPS * g + KT * (j + 1))
                act.wait_ge(o_normed, PRIMED + FINS * g + j)
                a(o_raw[:, :], oacc[:, 0:N], ACT.Copy).then_inc(o_saved, 1)

            def att_high(b, tc):
                i = tc % 2
                act.wait_ge(att_back[i], 16 * (CH // 2 * b + tc // 2 + 1))
                a(att_hi[i], att_in[i][:, :, :].bitcast(fp32), ACT.Copy).then_inc(att_hi_ready, 1)

            def pair(b, p, kp):
                g = pair_no(b, p)
                _, before, _ = PLANS[kp]
                for t in range(PSTEPS):
                    par = t // STEPS
                    act.wait_ge(pv_done, PRIMED + PSTEPS * g + max(0, t - RING + 1))
                    if t < RING:
                        if t == 0:
                            for e in range(2):
                                act.wait_ge(added[e], PRIMED + adds_in_pairs(e, g))
                    else:
                        e = adder(t - RING)
                        act.wait_ge(added[e], PRIMED + adds_in_pairs(e, g) + adds_by(t - RING))
                    act.wait_ge(scores_full, PSTEPS * g + t + 1)
                    a(probs[:, t % RING * QB:(t % RING + 1) * QB].rearrange("p (h n) -> p h n", n=N),
                      scores[:, t % 2, :, 0:N], ACT.Exp).then_inc(probs_ready, 1)
                    if t == 3:
                        for k in range(BANKS):
                            act.wait_ge(bank_free[k], uses_before(k, b, p))
                        a(v_odd[:, :, :], v_odd_next[:, :, :], ACT.Copy).then_inc(v_odd_ready, 1)
                    for kind, i in before[t]:
                        u = use(kp, b, p, use_key(par, kind, i)) if kind in POOLED else None
                        if kind == "prep":
                            head = (0 if kp == LAST else 2 * p + 2) if par else 2 * p + 1
                            prep(i, 1 - par, u, 2 * g + par + 1, head)
                        elif kind == "v":
                            v_group(i, u, g + 1)
                        elif kind == "maxrow":
                            max_row(u, 16 * (2 * g + par + 1))
                        elif kind == "finish":
                            save_sums(i, g, u)
                        elif kind == "sqrt":
                            sqrt(use(kp, b, p, ("groupvar", 0)))
                        elif kind == "normalize":
                            if i == (0, 0):
                                wait_full(act, use(kp, b, p, (0, "prep", CH - 1)))
                            normalize(*i, b + 1)
                    if t and t % KT == 0:
                        save_o(t // KT - 1, g)
                if kp != INNER:
                    att_high(b, 0)
                save_o(FINS - 1, g)
                save_sums(FINS - 1, g, use(kp, b, p, TAIL))

            def projection(b):
                att_high(b, 1)
                act.wait_ge(res_coefs_ready, b + 1)
                for n in range(PJ):
                    act.wait_ge(proj_full, PJ * b + n + 1)
                    if n >= 8:
                        act.wait_ge(out_ready, PRIMED + PJ * b + n - 7)
                    a(proj_sb[:, n % 8, :], scores[:, n // 2 % 2, n % 2, 0:N], ACT.Identity,
                      bias=res_b[:, n % CT:n % CT + 1]).then_inc(proj_saved, 1)
                    if n % CT == CT - 1 and n // CT + 2 < CH:
                        att_high(b, n // CT + 2)

            for s in (probs_ready, o_saved, proj_saved):
                act.sem_inc(s, PRIMED)
            sqrt(FIRST_USES["groupvar", 0])
            for part in range(BLOCKS):
                for i in range(CT):
                    normalize(i, part, 0)
            act.wait_ge(consts_made, 8)
            for (kind, i), u in FIRST_USES.items():
                if kind == "prep":
                    prep(i, 0, u, 0, 0)
                elif kind == "v":
                    v_group(i, u, None)
                    if i == 0:
                        act.wait_ge(wproj_in, 16)
                        a(wproj_hi[:, :, :], wproj_full, ACT.Copy).then_inc(wproj_hi_ready, 1)
                elif kind == "maxrow":
                    max_row(u, None)

            def batch(b, last_kind):
                for i in range(2):
                    act.wait_ge(stored[i], PRIMED + 16 * (CH // 2) * b)
                with act.Fori(0, PAIRS - 1) as p:
                    pair(b, p, INNER)
                pair(b, PAIRS - 1, last_kind)
                projection(b)

            with act.Fori(0, B - 1) as b:
                batch(b, LAST)
            batch(B - 1, END)

        @block.vector
        def _(dve):
            v = nc.vector
            NORM_LINKS = 7

            def low_parts(c, buf, u):
                cs = slice(c * N, (c + 1) * N)
                wait_free(dve, u)
                v.tensor_tensor(q_lo_max[buf][0:D, cs], qk_full[:, 0, :], q_hi_hi[buf][0:D, cs].bitcast(fp32),
                                ALU.subtract)
                v.tensor_tensor(k_hi_lo[buf][D:2 * D, cs], qk_full[:, 1, :], k_hi_lo[buf][0:D, cs].bitcast(fp32),
                                ALU.subtract).then_inc(lo_ready, 1)

            def unit_max(n, u, heads_done):
                wait_full(dve, u)
                if n == 0 and heads_done is not None:
                    dve.wait_ge(neg_ready, heads_done)
                v.tensor_reduce(maxima[:, n:n + 1], pool_banks[:, u[0], 0:N], AX.X, ALU.max)\
                 .then_inc(bank_free[u[0]], 1)

            def negate_max(last_unit, last_row):
                wait_free(dve, last_unit)
                if last_row is not None:
                    wait_full(dve, last_row)
                v.tensor_reduce(neg_max[:, :], maxima[:, :].rearrange("p (q c) -> p q c", c=CH), AX.X,
                                ALU.max, negate=True).then_inc(neg_ready, 1)

            def take_stats(i, part, k):
                if first_batch(k):
                    tile = xn[:, i, :]
                    if part == 0:
                        dve.wait_ge(x0_in[i], 16)
                else:
                    tile = xtile[:, :]
                    dve.wait_ge(x_in[part], 16 * (2 * CT * (k - 1) + i + 1))
                if part == 0 and (i or not first_batch(k)):
                    dve.wait_ge(stats_done, CT * k + i)
                for c in range(2 * part, 2 * part + 2):
                    last = v.bn_stats(stats[:, c, :], tile[:, c * N:(c + 1) * N])
                last.then_inc(stats_taken, 1)
                if part == BLOCKS - 1:
                    dve.wait_ge(stats_taken, BLOCKS * (CT * k + i + 1))
                    v.memset(spare[:, :], 0.0)
                    v.bn_aggr(meanvar[:, i, :], stats[:, :, :]).then_inc(stats_done, 1)

            def link(ins, n):
                ins.then_inc(chain, 1)
                dve.wait_ge(chain, n)

            def deviations(k, u):
                at = NORM_LINKS * k
                wait_full(dve, u)
                if not first_batch(k):
                    dve.wait_ge(coefs_ready, k)
                v.tensor_tensor(dev, meanvar[:, :, 0], pool_banks[:, u[0], 0:CT], ALU.subtract)
                v.tensor_copy(gmean, pool_banks[:, u[0], 0:CT]).then_inc(bank_free[u[0]], 1)
                wait_free(dve, u)
                link(v.tensor_tensor(inv, dev, dev, ALU.mult), at + 1)
                v.tensor_tensor(tmp, inv, meanvar[:, :, 1], ALU.add).then_inc(dev_ready, 1)

            def group_variance(u):
                wait_full(dve, u)
                v.tensor_scalar_add(gvar, pool_banks[:, u[0], 0:CT], EPS).then_inc(bank_free[u[0]], 1)

            def coefs(k):
                at = NORM_LINKS * k + 1
                dve.wait_ge(root_ready, k + 1)
                dve.wait_ge(dev_ready, k + 1)
                link(v.reciprocal(inv, root), at + 1)
                link(v.tensor_tensor(tmp, inv, inv, ALU.mult), at + 2)
                link(v.tensor_tensor(tmp, tmp, gvar, ALU.mult), at + 3)
                link(v.tensor_scalar(tmp, tmp, -0.5, 1.5, ALU.mult, ALU.add), at + 4)
                link(v.tensor_tensor(inv, inv, tmp, ALU.mult), at + 5)
                if not first_batch(k):
                    dve.wait_ge(res_coefs_ready, k)
                v.tensor_tensor(next_a, inv, gw, ALU.mult).then_inc(chain, 1)
                dve.wait_ge(chain, at + 6)
                v.tensor_tensor(tmp, gmean, next_a, ALU.mult).then_inc(shift_ready, 1)
                dve.wait_ge(shift_ready, k + 1)
                v.tensor_tensor(next_b, gb, tmp, ALU.subtract).then_inc(coefs_ready, 1)

            def add(t, g):
                kt, j = t % KT, t // KT
                tiles = ADDED[j % BLOCKS][0]
                if kt not in tiles[1:]:
                    return
                i = tiles.index(kt)
                dve.wait_ge(probs_ready, PRIMED + PSTEPS * g + t + 1)
                acc = denom[:, j % 2, 0, :]
                now = probs[:, t % RING * QB:(t % RING + 1) * QB]
                if i == 1:
                    t0 = t - kt + tiles[0]
                    first = probs[:, t0 % RING * QB:(t0 % RING + 1) * QB]
                    v.tensor_tensor(acc, first, now, ALU.add).then_inc(added[0], 1)
                else:
                    dve.wait_ge(added[0], PRIMED + adds_in_pairs(0, g) + adds_by(t) - 1)
                    v.tensor_tensor(acc, acc, now, ALU.add).then_inc(added[0], 1)

            def take_recip(j, g, u, pieces, of):
                for i in pieces:
                    cs = slice(i * N // of, (i + 1) * N // of)
                    if i == 0:
                        wait_free(dve, u)
                        dve.wait_ge(o_normed, PRIMED + FINS * g + j)
                    last = v.reciprocal(recip[:, cs], sums[:, cs])
                if i == of - 1:
                    last.then_inc(recip_ready, 1)
                    dve.wait_ge(recip_ready, FINS * g + j + 1)
                    dve.wait_ge(o_saved, PRIMED + FINS * g + j + 1)
                    dve.wait_ge(att_out, PRIMED + 32 * (FINS * g + j))
                    v.tensor_tensor(o_norm[:, :], o_raw[:, :], recip[:, :], ALU.mult).then_inc(o_normed, 1)

            def att_low(b, tc):
                i = tc % 2
                dve.wait_ge(att_hi_ready, CH * b + tc + 1)
                v.tensor_tensor(att_in[i][:, :, :], att_in[i][:, :, :].bitcast(fp32), att_hi[i].bitcast(fp32),
                                ALU.subtract).then_inc(att_lo_ready, 1)

            def pair(b, p, kp):
                g = pair_no(b, p)
                within, before, after = PLANS[kp]
                for t in range(PSTEPS):
                    par = t // STEPS
                    done = 2 * g + par + 1
                    for kind, i in within[t] + before[t]:
                        if kind == "aux":
                            unit_max(i, use(kp, b, p, (par, kind, i)), done)
                        elif kind == "maxrow":
                            negate_max(use(kp, b, p, (par, "aux", UNITS - 1)),
                                       use(kp, b, p, (0, "maxrow", 0)) if par else None)
                    add(t, g)
                    for kind, i in before[t]:
                        u = use(kp, b, p, use_key(par, kind, i)) if kind in POOLED else None
                        if kind == "prep":
                            low_parts(i, 1 - par, u)
                        elif kind == "finish" and i % BLOCKS == BLOCKS - 1:
                            take_recip(i, g, u, (0,), 1)
                        elif kind == "recip":
                            j, piece = i
                            take_recip(j, g, use(kp, b, p, ("finish", j)), (piece,), PIECES)
                        elif kind == "stats":
                            take_stats(*i, b + 1)
                        elif kind == "groupmean":
                            deviations(b + 1, u)
                        elif kind == "groupvar":
                            group_variance(u)
                        elif kind == "coefs":
                            coefs(b + 1)
                    for _, i in after[t]:
                        unit_max(i, use(kp, b, p, (par, "aux", i)), done)
                if kp != INNER:
                    att_low(b, 0)
                take_recip(FINS - 1, g, use(kp, b, p, TAIL), (0,), 1)

            def projection(b):
                att_low(b, 1)
                for n in range(PJ):
                    tc, ot = n // CT, n % CT
                    i = tc % 2
                    if ot == 0 and 0 < tc < CH - 1:
                        att_low(b, tc + 1)
                    if ot == 0:
                        dve.wait_ge(xres_in[i], 16 * (CH // 2 * b + tc // 2 + 1))
                    dve.wait_ge(proj_saved, PRIMED + PJ * b + n + 1)
                    tile = xres(i)[:, ot, :]
                    v.scalar_tensor_tensor(tile, tile, res_a[:, ot:ot + 1], proj_sb[:, n % 8, :],
                                           ALU.mult, ALU.add).then_inc(out_ready, 1)

            for s in (added[0], o_normed, out_ready):
                dve.sem_inc(s, PRIMED)
            v.memset(ones[:, :], 1.0).then_inc(consts_made, 1)
            for i in range(2):
                v.memset(k_hi_one[i][D:D + 1, :].bitcast(fp32), 1.0).then_inc(consts_made, 1)
            for i in range(CT):
                for part in range(BLOCKS):
                    take_stats(i, part, 0)
            deviations(0, FIRST_USES["groupmean", 0])
            group_variance(FIRST_USES["groupvar", 0])
            dve.wait_ge(consts_in, 80)
            v.tensor_scalar(bqk_s[:, :], bqk_s[:, :], QK_SCALE, None, ALU.mult).then_inc(consts_made, 1)
            coefs(0)
            u = FIRST_USES["bias", 0]
            wait_full(dve, u)
            v.tensor_tensor(pb, pb, pool_banks[:, u[0], 0:CT], ALU.add).then_inc(bank_free[u[0]], 1)
            for (kind, i), u in FIRST_USES.items():
                if kind == "prep":
                    low_parts(i, 0, u)
                elif kind == "aux":
                    unit_max(i, u, None)
            negate_max(FIRST_USES["aux", UNITS - 1], None)
            dve.wait_ge(wproj_hi_ready, 1)
            v.tensor_tensor(wproj_lo[:, :, :], wproj_full, wproj_hi[:, :, :].bitcast(fp32),
                            ALU.subtract).then_inc(wproj_lo_ready, 1)

            def batch(b, last_kind):
                dve.wait_ge(coefs_ready, b + 1)
                dve.wait_ge(out_ready, PRIMED + PJ * b)
                dve.wait_ge(proj_saved, PRIMED + PJ * b)
                wait_free(dve, FIRST_USES["bias", 0])
                v.tensor_copy(res_a, next_a)
                v.tensor_tensor(res_b, next_b, pb, ALU.add).then_inc(res_coefs_ready, 1)
                with dve.Fori(0, PAIRS - 1) as p:
                    pair(b, p, INNER)
                pair(b, PAIRS - 1, last_kind)
                projection(b)

            with dve.Fori(0, B - 1) as b:
                batch(b, LAST)
            batch(B - 1, END)

        @block.gpsimd
        def _(pool):
            gp = nc.gpsimd

            def add(t, g):
                kt, j = t % KT, t // KT
                tiles = ADDED[j % BLOCKS][1]
                if kt not in tiles[1:]:
                    return
                i = tiles.index(kt)
                pool.wait_ge(probs_ready, PRIMED + PSTEPS * g + t + 1)
                acc = denom[:, j % 2, 1, :]
                now = probs[:, t % RING * QB:(t % RING + 1) * QB]
                if i == 1:
                    t0 = t - kt + tiles[0]
                    first = probs[:, t0 % RING * QB:(t0 % RING + 1) * QB]
                    if j >= 2:
                        pool.wait_ge(o_normed, PRIMED + FINS * g + j - 1)
                    gp.tensor_tensor(acc, first, now, ALU.add).then_inc(added[1], 1)
                else:
                    pool.wait_ge(added[1], PRIMED + adds_in_pairs(1, g) + adds_by(t) - 1)
                    gp.tensor_tensor(acc, acc, now, ALU.add).then_inc(added[1], 1)

            def merge(j, g):
                pool.wait_ge(added[0], PRIMED + adds_in_pairs(0, g) + adds_before(0, j + 1))
                pool.wait_ge(added[1], PRIMED + adds_in_pairs(1, g) + adds_before(1, j + 1))
                gp.tensor_tensor(denom[:, j % 2, 1, :], denom[:, j % 2, 1, :], denom[:, j % 2, 0, :],
                                 ALU.add).then_inc(merged, 1)

            def pair(b, p, kp):
                g = pair_no(b, p)
                pool.wait_ge(out_ready, PRIMED + PJ * b)
                pool.wait_ge(o_normed, PRIMED + FINS * g)
                for t in range(PSTEPS):
                    add(t, g)
                    if t and t % KT == 0:
                        merge(t // KT - 1, g)

            pool.sem_inc(added[1], PRIMED)
            gp.memset(ident[:, :], 0.0).then_inc(masks_filled, 1)
            gp.memset(groups[:, :], 1.0 / GROUP).then_inc(masks_filled, 1)
            pool.wait_ge(masks_filled, 2)
            gp.affine_select(out=ident[:, :], in_=ident[:, :], compare_op=ALU.not_equal, fill=1.0,
                             base=0, pattern=[[-1, 128]], channel_multiplier=1).then_inc(consts_made, 2)
            gv = groups[:, :].rearrange("p (g c) -> p g c", c=GROUP)
            gp.affine_select(out=gv, in_=gv, compare_op=ALU.is_ge, fill=0.0, base=0,
                             pattern=[[-GROUP, 128 // GROUP], [0, GROUP]], channel_multiplier=1)\
              .then_inc(masks_filled, 1)
            pool.wait_ge(masks_filled, 3)
            gp.affine_select(out=gv, in_=gv, compare_op=ALU.is_ge, fill=0.0, base=GROUP - 1,
                             pattern=[[GROUP, 128 // GROUP], [0, GROUP]], channel_multiplier=-1)\
              .then_inc(consts_made, 2)

            def batch(b, last_kind):
                with pool.Fori(0, PAIRS - 1) as p:
                    pair(b, p, INNER)
                pair(b, PAIRS - 1, last_kind)

            with pool.Fori(0, B - 1) as b:
                batch(b, LAST)
            batch(B - 1, END)


def kernel(**inputs):
    import numpy as np
    import concourse.bacc as bacc
    from concourse import mybir
    from concourse.bass_utils import run_bass_kernel_spmd

    x = np.asarray(inputs["x"])
    B, C, HH, WW = x.shape
    H, CT = 8, C // 128
    D = C // H
    bqkv = np.asarray(inputs["L0_conv_qkv_b"]).reshape(H, 3 * D)

    def columns(v):
        return np.ascontiguousarray(np.asarray(v).reshape(CT, 128).T)

    arrays = {
        "x": np.ascontiguousarray(x.reshape(B, C, HH * WW)),
        "gn_w": columns(inputs["L0_conv_gn_w"]),
        "gn_b": columns(inputs["L0_conv_gn_b"]),
        "wqkv_t": np.ascontiguousarray(np.asarray(inputs["L0_conv_qkv_w"]).T).reshape(C, H, 3 * D),
        "bqk": np.ascontiguousarray(bqkv[:, :2 * D].T),
        "bv": columns(bqkv[:, 2 * D:]),
        "wproj_t": np.ascontiguousarray(np.asarray(inputs["L0_conv_proj_w"]).T),
        "bproj": columns(inputs["L0_conv_proj_b"]),
    }
    nc = bacc.Bacc("TRN2", target_bir_lowering=False, num_devices=1)
    fp32 = mybir.dt.float32
    aps = {n: nc.dram_tensor(n, v.shape, mybir.dt.from_np(v.dtype), kind="ExternalInput").ap()
           for n, v in arrays.items()}
    att = nc.dram_tensor("att", (CT, 128, HH * WW), fp32, kind="Internal").ap()
    out = nc.dram_tensor("out", (B, C, HH * WW), fp32, kind="ExternalOutput").ap()
    attention_block_program(nc, att=att, out=out, **aps)
    r = run_bass_kernel_spmd(nc, [arrays], core_ids=[0])
    return r.results[0]["out"].reshape(B, C, HH, WW)
```
